# Optimizing a Trainium2 kernel written in Bass

```python
import numpy as np
import jax
import jax.numpy as jnp

def _softmax(x, axis=-1):
    return jax.nn.softmax(x, axis=axis)

def _gelu(x):
    return jax.nn.gelu(x, approximate=True)

def _silu(x):
    return jax.nn.silu(x)

def _sigmoid(x):
    return jax.nn.sigmoid(x)

def _layernorm(x, axis=-1, eps=1e-05):
    m = jnp.mean(x, axis=axis, keepdims=True)
    v = jnp.var(x, axis=axis, keepdims=True)
    return (x - m) / jnp.sqrt(v + eps)

def _scatter_add(tgt, idx, src, axis=0):
    return tgt.at[idx].add(src)

def _segment_sum(src, seg, n):
    return jax.ops.segment_sum(src, seg, n)
kernel_name = 'mk_prb_d1_jaxref_r4_0ad9c4'

def setup_inputs(seed: int=0):
    np.random.seed(seed)
    _w = jnp.asarray

    def _L0_attn_setup():
        import jax, jax.numpy as jnp
        import numpy as np
        NUM_HEADS = 16
        PHI = 1.6180339887
        STRIDE = 4
        LOCAL = 8

        def _strided_allowed(S):
            i = jnp.arange(S)[:, None]
            j = jnp.arange(S)[None, :]
            return (j % STRIDE == 0) | (jnp.abs(i - j) <= LOCAL)
        key = jax.random.key(seed)
        ks = jax.random.split(key, 6)
        B, S, H = (2, 512, 256)
        scale = H ** (-0.5)
        x = jax.random.normal(ks[0], (B, S, H), jnp.float32)
        q_w = jax.random.normal(ks[1], (H, H), jnp.float32) * scale
        k_w = jax.random.normal(ks[2], (H, H), jnp.float32) * scale
        v_w = jax.random.normal(ks[3], (H, H), jnp.float32) * scale
        o_w = jax.random.normal(ks[4], (H, H), jnp.float32) * scale
        o_b = jax.random.normal(ks[5], (H,), jnp.float32) * 0.01
        unity_scale = jnp.asarray(PHI, jnp.float32)
        return {'x': x, 'q_w': q_w, 'k_w': k_w, 'v_w': v_w, 'o_w': o_w, 'o_b': o_b, 'unity_scale': unity_scale}
    _L0_attn_in = _L0_attn_setup()

    def _L0_ffn_setup():
        import jax, jax.numpy as jnp
        import numpy as np
        FP8_MAX = 448.0
        key = jax.random.key(seed)
        k_x, k_w, k_b = jax.random.split(key, 3)
        B, S, IN, OUT = (4, 2048, 256, 256)
        x = jax.random.normal(k_x, (B, S, IN), dtype=jnp.float32)
        w_fp32 = jax.random.normal(k_w, (OUT, IN), dtype=jnp.float32)
        weight_fp8 = w_fp32.astype(jnp.float8_e4m3fn).astype(jnp.float32)
        bias = jax.random.normal(k_b, (OUT,), dtype=jnp.float32)
        input_scale = jnp.ones((1,), dtype=jnp.float32)
        weight_scale = jnp.ones((1,), dtype=jnp.float32)
        return {'x': x, 'weight_fp8': weight_fp8, 'bias': bias, 'input_scale': input_scale, 'weight_scale': weight_scale}
    _L0_ffn_in = _L0_ffn_setup()
    _d = {'L0_attn_x': _L0_attn_in['x'], 'L0_attn_q_w': _L0_attn_in['q_w'], 'L0_attn_k_w': _L0_attn_in['k_w'], 'L0_attn_v_w': _L0_attn_in['v_w'], 'L0_attn_o_w': _L0_attn_in['o_w'], 'L0_attn_o_b': _L0_attn_in['o_b'], 'L0_attn_unity_scale': _L0_attn_in['unity_scale'], 'L0_ffn_weight_fp8': _L0_ffn_in['weight_fp8'], 'L0_ffn_bias': _L0_ffn_in['bias'], 'L0_ffn_input_scale': _L0_ffn_in['input_scale'], 'L0_ffn_weight_scale': _L0_ffn_in['weight_scale']}
    _x0 = _d['L0_attn_x']
    _d['L0_attn_x'] = jax.random.normal(jax.random.fold_in(jax.random.key(seed), 1), (4, 2048, 256), dtype=_x0.dtype)
    del _x0
    return _d

def reference(L0_attn_x, L0_attn_q_w, L0_attn_k_w, L0_attn_v_w, L0_attn_o_w, L0_attn_o_b, L0_attn_unity_scale, L0_ffn_weight_fp8, L0_ffn_bias, L0_ffn_input_scale, L0_ffn_weight_scale):

    def _L0_attn_ref(x, q_w, k_w, v_w, o_w, o_b, unity_scale):
        import jax, jax.numpy as jnp
        import numpy as np
        NUM_HEADS = 16
        PHI = 1.6180339887
        STRIDE = 4
        LOCAL = 8

        def _strided_allowed(S):
            i = jnp.arange(S)[:, None]
            j = jnp.arange(S)[None, :]
            return (j % STRIDE == 0) | (jnp.abs(i - j) <= LOCAL)
        B, S, H = x.shape
        NH = NUM_HEADS
        D = H // NH
        q = (x @ q_w).reshape(B, S, NH, D).transpose(0, 2, 1, 3)
        k = (x @ k_w).reshape(B, S, NH, D).transpose(0, 2, 1, 3)
        v = (x @ v_w).reshape(B, S, NH, D).transpose(0, 2, 1, 3)
        q = q * jax.nn.sigmoid(unity_scale)
        scores = jnp.einsum('bhqd,bhkd->bhqk', q, k) / jnp.sqrt(jnp.asarray(D, x.dtype))
        allowed = _strided_allowed(S)
        scores = jnp.where(allowed, scores, -jnp.inf)
        attn = jax.nn.softmax(scores, axis=-1)
        out = jnp.einsum('bhqk,bhkd->bhqd', attn, v)
        out = out.transpose(0, 2, 1, 3).reshape(B, S, H)
        return out @ o_w + o_b

    def _L0_ffn_ref(x, weight_fp8, bias, input_scale, weight_scale):
        import jax, jax.numpy as jnp
        import numpy as np
        FP8_MAX = 448.0
        x_q = jnp.clip(x / input_scale, -FP8_MAX, FP8_MAX)
        x_dq = x_q.astype(jnp.float8_e4m3fn).astype(x.dtype) * input_scale
        w_dq = weight_fp8 * weight_scale
        out = jnp.einsum('bsi,oi->bso', x_dq, w_dq) + bias
        return out
    x = L0_attn_x
    xn = _layernorm(x, axis=-1)
    x = x + _L0_attn_ref(xn, L0_attn_q_w, L0_attn_k_w, L0_attn_v_w, L0_attn_o_w, L0_attn_o_b, L0_attn_unity_scale) + _L0_ffn_ref(xn, L0_ffn_weight_fp8, L0_ffn_bias, L0_ffn_input_scale, L0_ffn_weight_scale)
    return x

_drawn_inputs = setup_inputs


def setup_inputs(seed=0):
    import zlib

    import numpy as np

    out = dict(_drawn_inputs(seed))
    spreads = {}
    factors = {'L0_attn_q_w': 8.0,
     'L0_attn_k_w': 8.0,
     'L0_attn_v_w': 8.0,
     'L0_attn_o_w': 8.0,
     'L0_attn_o_b': 200.0,
     'L0_ffn_bias': 3.561}
    for name, (base, spread) in spreads.items():
        noise = np.random.default_rng([zlib.crc32(name.encode()), seed]).standard_normal(out[name].shape)
        drawn = base * np.exp(spread * noise) if base else spread * noise
        out[name] = jnp.asarray(drawn.astype(out[name].dtype))
    for name, factor in factors.items():
        out[name] = (out[name] * factor).astype(out[name].dtype)
    return out
```

```python
from contextlib import ExitStack

import concourse.bass as bass
from concourse import mybir

F32 = mybir.dt.float32
BF16 = mybir.dt.bfloat16
I32 = mybir.dt.int32
ALU = mybir.AluOpType
ACT = mybir.ActivationFunctionType
AX_X = mybir.AxisListType.X

B, S, H = 4, 2048, 256
NH, D = 16, 16
P = 128
KC = H // P
CH = 512
TT = CH // P
CPB = S // CH
G, HG = 4, 4
NIT = B * G
STEPS = NIT * CPB
STRIDE, LOCAL = 4, 8
NS = S // STRIDE
WIN = (P + 2 * LOCAL) // STRIDE * (STRIDE - 1)
WSTEP = P // STRIDE * (STRIDE - 1)
WPAD = LOCAL // STRIDE * (STRIDE - 1)
PARTS = 3
KR = 6 * D
KM = KR + PARTS
VW = 32
EPS = 1e-5
FP8_MAX = 448.0
FP8_MIN_NORMAL = 2.0 ** -6
ROUND = 1.5 * 2.0 ** 20
BIG = 1e30
MASKS = 3


def part_project(nc, io, dram, keep):
    with ExitStack() as ctx:
        def sb(name, shape, dt=F32):
            return ctx.enter_context(nc.sbuf_tensor(name, shape, dt))

        def sem(name):
            return ctx.enter_context(nc.semaphore(name))

        ps = ctx.enter_context(nc.psum_tensor("ps_project", [P, 8, CH], F32))
        ps_q, ps_t, ps_k, ps_v = (ps[:, 2 * i:2 * i + 2, :] for i in range(4))
        ps_f = ps_t

        wq, wk, wv = (sb(n, [P, KC, H]) for n in ("wq", "wk", "wv"))
        w8 = sb("w8", [P, KC, H])
        w8_rest = sb("w8_rest", [P, KC, H])
        w8_parts = sb("w8_parts", [P, PARTS, KC, H], BF16)
        bias = sb("bias", [P, H])
        bias_o = sb("bias_o", [P, H])
        scales = sb("scales", [P, 3])
        zeros = sb("zeros", [NIT, LOCAL * HG * VW])
        x_in = sb("x_in", [P, 2, TT, H])
        stats = sb("stats", [P, TT, 6])
        counts = sb("counts", [P, TT])
        mv = sb("mv", [P, TT, 2])
        var = sb("var", [P, TT])
        dev = sb("dev", [P, TT])
        newton = sb("newton", [P, 3, TT])
        rstd = sb("rstd", [P, TT])
        xn = sb("xn", [P, 2, TT, H])
        xnT = sb("xnT", [P, 2, KC, CH])
        qk_parts = sb("qk_parts", [P, 2, 2, PARTS, KC, CH], BF16)
        rest = sb("rest", [P, 2, KC, CH])
        v_sb = sb("v_sb", [P, 2, TT, NH, VW])
        quant = sb("quant", [P, KC, CH])
        power = sb("power", [P, KC, CH])
        y8 = sb("y8", [P, 2, KC, CH], BF16)
        xb = sb("xb", [P, TT, H])
        base = sb("base", [P, 2, TT, H])

        w_loaded = sem("w_loaded")
        c_loaded = sem("c_loaded")
        zeros_set = sem("zeros_set")
        v_set = sem("v_set")
        pads_stored = sem("pads_stored")
        setup = sem("setup")
        w8_ready = sem("w8_ready")
        bias_ready = sem("bias_ready")
        x_loaded = [sem(f"x_loaded{i}") for i in range(2)]
        stat = sem("stat")
        var_ready = sem("var_ready")
        dev_ready = sem("dev_ready")
        xn_ready = sem("xn_ready")
        t_ready = sem("t_ready")
        xnT_ready = sem("xnT_ready")
        q_ready = sem("q_ready")
        k_ready = sem("k_ready")
        v_ready = sem("v_ready")
        f_ready = sem("f_ready")
        hi_ready = sem("hi_ready")
        rest_ready = sem("rest_ready")
        mid_ready = sem("mid_ready")
        lo_ready = sem("lo_ready")
        v_copied = sem("v_copied")
        quant_chain = sem("quant_chain")
        power_ready = sem("power_ready")
        sum_ready = sem("sum_ready")
        y8_ready = sem("y8_ready")
        xb_ready = sem("xb_ready")
        base_ready = sem("base_ready")
        qk_stored = [sem(f"qk_stored{i}") for i in range(2)]
        v_stored = [sem(f"v_stored{i}") for i in range(2)]
        base_stored = [sem(f"base_stored{i}") for i in range(2)]

        x_rows = io["x"].rearrange("b (c t p) f -> (b c) p t f", t=TT, p=P)
        base_rows = dram["base"].rearrange("(c t p) f -> c p t f", t=TT, p=P)
        block = ctx.enter_context(nc.Block())

        def half(j, n):
            return CPB // 2 * j + n // 2

        def chunks(eng, body):
            for n in range(-1, 3):
                body(0, n)
            with eng.Fori(0, B - 2) as j:
                for n in range(3, 3 + CPB):
                    body(j, n)
            for n in range(B * CPB - CPB - 1, B * CPB):
                body(0, n)

        @block.sync
        def _(sp):
            sp.dma_start(keep["ident"][:], io["ident"]).then_inc(c_loaded, 16)
            sp.dma_start(x_in[:, 0], x_rows[0]).then_inc(x_loaded[0], 16)
            sp.dma_start(scales[:, 0:1], io["input_scale"].partition_broadcast(P)).then_inc(c_loaded, 16)
            sp.dma_start(scales[:, 1:2], io["weight_scale"].partition_broadcast(P)).then_inc(c_loaded, 16)
            sp.dma_start(w8[:], io["w8T"].rearrange("(k p) f -> p k f", p=P)).then_inc(c_loaded, 16)
            sp.dma_start(bias[:], io["ffn_bias"].partition_broadcast(P)).then_inc(c_loaded, 16)
            sp.dma_start(bias_o[:], io["o_b"].partition_broadcast(P)).then_inc(c_loaded, 16)
            for w, name in ((wq, "q_w"), (wk, "k_w"), (wv, "v_w")):
                sp.dma_start(w[:], io[name].rearrange("(k p) f -> p k f", p=P)).then_inc(w_loaded, 16)
            sp.dma_start(keep["unity"][:], io["unity"].partition_broadcast(P)).then_inc(c_loaded, 16)
            sp.dma_start(keep["max_mask_f"][:], io["max_mask"].rearrange("m p n -> p m n")).then_inc(c_loaded, 16)
            sp.dma_start(keep["key_mask_f"][0:WIN], io["key_mask"].rearrange("m p n -> p m n")).then_inc(c_loaded, 16)
            sp.dma_start(keep["wo"][:], io["o_w"].rearrange("(k p) f -> p k f", p=P)).then_inc(c_loaded, 16)
            sp.wait_ge(zeros_set, 1)
            for edge in (0, LOCAL + S):
                sp.dma_start(dram["v"][:, edge:edge + LOCAL, :], zeros[:]).then_inc(pads_stored, 16)

            def body(j, n):
                c = CPB * j + n
                if n >= -1 and not (isinstance(c, int) and c + 2 > B * CPB - 1):
                    if n >= 0:
                        sp.wait_ge(xn_ready, c + 1)
                        sp.wait_ge(xb_ready, c + 1)
                    if n >= 0:
                        sp.dma_start(x_in[:, n % 2], x_rows[c + 2]).then_inc(x_loaded[n % 2], 16)
                    else:
                        sp.dma_start(x_in[:, 1], x_rows[1]).then_inc(x_loaded[1], 16)
                if isinstance(c, int) and c < 0:
                    return
                b4, cq, k = (j + n // CPB) * G, n % CPB, n % 2
                for w in range(2):
                    sp.wait_ge(lo_ready, 2 * c + w + 1)
                    for part in range(PARTS):
                        for side in range(2):
                            rows = slice(64 * side, 64 * side + 64)
                            ns = CH // STRIDE if w else 0
                            spans = [(cq * CH, 0, CH)] if not w else [
                                (cq * ns, 0, ns), (NS + cq * (CH - ns), ns, CH)]
                            for to, a, e in spans:
                                sp.dma_start(
                                    dram["qk"][w][bass.ds(b4 + side, 2, step=2), part, :, to:to + e - a]
                                    .rearrange("m r s -> r m s"),
                                    qk_parts[rows, k, w, part, :, a:e]).then_inc(qk_stored[k], 16)
                sp.wait_ge(v_copied, c + 1)
                for t in range(TT):
                    row = LOCAL + cq * CH + t * P
                    sp.dma_start(dram["v"][bass.ds(b4, G), row:row + P, :].rearrange("g p w -> p g w"),
                                 v_sb[:, k, t].rearrange("p (g h) w -> p g (h w)", g=G)).then_inc(v_stored[k], 16)
                sp.wait_ge(base_ready, c + 1)
                sp.dma_start(base_rows[c], base[:, k]).then_inc(base_stored[k], 16)

            chunks(sp, body)
            sp.wait_ge(pads_stored, 32)
            for k in range(2):
                sp.wait_ge(qk_stored[k], 16 * 18 * B * CPB // 2)
                sp.wait_ge(v_stored[k], 16 * TT * B * CPB // 2)
                sp.wait_ge(base_stored[k], 16 * B * CPB // 2)

        @block.gpsimd
        def _(pool):
            nc.gpsimd.memset(zeros[:], 0.0).then_inc(zeros_set, 1)
            nc.gpsimd.memset(v_sb[:, 0, :, :, D:VW], 0.0).then_inc(v_set, 1)
            nc.gpsimd.memset(v_sb[:, 1, :, :, D:VW], 0.0).then_inc(v_set, 1)
            pool.wait_ge(v_set, 2)
            nc.gpsimd.memset(v_sb[:, 0, :, :, D:D + 1], 1.0).then_inc(v_set, 1)
            nc.gpsimd.memset(v_sb[:, 1, :, :, D:D + 1], 1.0).then_inc(v_set, 1)
            pool.wait_ge(bias_ready, 1)

            def body(j, n):
                c = CPB * j + n
                if isinstance(c, int) and c < 0:
                    return
                k = n % 2
                pool.wait_ge(x_loaded[k], 16 * (half(j, n) + 1))
                if not (isinstance(c, int) and c < 1):
                    pool.wait_ge(base_ready, c)
                nc.gpsimd.tensor_tensor(xb[:], x_in[:, k], bias[:].unsqueeze(1).broadcast_to([P, TT, H]),
                                        ALU.add).then_inc(xb_ready, 1)
                pool.wait_ge(power_ready, c + 1)
                nc.gpsimd.tensor_tensor(quant[:], quant[:], power[:], ALU.add).then_inc(sum_ready, 1)
                pool.wait_ge(sum_ready, c + 1)
                if not (isinstance(c, int) and c < 2):
                    pool.wait_ge(f_ready, c - 1)
                nc.gpsimd.tensor_tensor(y8[:, k], quant[:], power[:], ALU.subtract).then_inc(y8_ready, 1)

            chunks(pool, body)

        @block.scalar
        def _(act):
            def body(j, n):
                c = CPB * j + n
                k = n % 2
                main = not (isinstance(c, int) and c < 0)
                ahead = not (isinstance(c, int) and c + 1 > B * CPB - 1)
                if ahead:
                    act.wait_ge(var_ready, c + 2)
                    nc.scalar.activation(dev[:], var[:], ACT.Sqrt).then_inc(dev_ready, 1)
                if main:
                    act.wait_ge(q_ready, c + 1)
                    if not (isinstance(c, int) and c < 2):
                        act.wait_ge(qk_stored[k], 16 * 18 * half(j, n))
                    nc.scalar.activation(qk_parts[:, k, 0, 0], ps_q, ACT.Copy).then_inc(hi_ready, 1)
                if ahead:
                    act.wait_ge(t_ready, c + 2)
                    if not (isinstance(c, int) and c < 1):
                        act.wait_ge(v_ready, c)
                        act.wait_ge(power_ready, c)
                    nc.scalar.activation(xnT[:, (n + 1) % 2], ps_t, ACT.Copy).then_inc(xnT_ready, 1)
                if main:
                    act.wait_ge(k_ready, c + 1)
                    nc.scalar.activation(qk_parts[:, k, 1, 0], ps_k, ACT.Copy).then_inc(hi_ready, 1)
                    act.wait_ge(rest_ready, 2 * c + 1)
                    nc.scalar.activation(qk_parts[:, k, 0, 1], rest[:, 0], ACT.Copy).then_inc(mid_ready, 1)
                    act.wait_ge(v_ready, c + 1)
                    if isinstance(c, int) and c == 0:
                        act.wait_ge(v_set, 4)
                    if not (isinstance(c, int) and c < 2):
                        act.wait_ge(v_stored[k], 16 * TT * half(j, n))
                    nc.scalar.activation(
                        v_sb[:, k].rearrange("p t h w -> p (t h) w")[:, :, 0:D],
                        ps_v.rearrange("p a (t w) -> p (a t) w", w=D), ACT.Copy).then_inc(v_copied, 1)
                    act.wait_ge(rest_ready, 2 * c + 2)
                    nc.scalar.activation(qk_parts[:, k, 1, 1], rest[:, 1], ACT.Copy).then_inc(mid_ready, 1)

            chunks(act, body)

        @block.vector
        def _(dve):
            dve.wait_ge(c_loaded, 16 * 10)
            nc.vector.tensor_copy(keep["max_mask"][:], keep["max_mask_f"][:])
            nc.vector.tensor_copy(keep["key_mask"][0:WIN], keep["key_mask_f"][0:WIN])
            nc.vector.tensor_copy(keep["ident_bf"][:], keep["ident"][:])
            nc.vector.reciprocal(scales[:, 2:3], scales[:, 0:1])
            nc.vector.tensor_tensor(bias[:], bias[:], bias_o[:], ALU.add).then_inc(bias_ready, 1)
            nc.vector.tensor_scalar(w8[:], w8[:], scales[:, 1:2], scales[:, 0:1], ALU.mult, ALU.mult).then_inc(setup, 1)
            dve.wait_ge(setup, 1)
            nc.vector.tensor_copy(w8_parts[:, 0], w8[:]).then_inc(setup, 1)
            dve.wait_ge(setup, 2)
            nc.vector.tensor_tensor(w8_rest[:], w8[:], w8_parts[:, 0], ALU.subtract).then_inc(setup, 1)
            dve.wait_ge(setup, 3)
            nc.vector.tensor_copy(w8_parts[:, 1], w8_rest[:]).then_inc(setup, 1)
            dve.wait_ge(setup, 4)
            nc.vector.tensor_tensor(w8_parts[:, 2], w8_rest[:], w8_parts[:, 1], ALU.subtract).then_inc(w8_ready, 1)

            def body(j, n):
                c = CPB * j + n
                k, k1 = n % 2, (n + 1) % 2
                main = not (isinstance(c, int) and c < 0)
                ahead = not (isinstance(c, int) and c + 1 > B * CPB - 1)
                done = 6 * (c + 1)
                if ahead:
                    dve.wait_ge(x_loaded[k1], 16 * (half(j, n + 1) + 1))
                    for t in range(TT):
                        last = nc.vector.bn_stats(stats[:, t], x_in[:, k1, t])
                    last.then_inc(stat, 1)
                    dve.wait_ge(stat, done + 1)
                    nc.vector.tensor_copy(counts[:], stats[:, :, 0])
                    for t in range(TT):
                        last = nc.vector.bn_aggr(mv[:, t], stats[:, t])
                    last.then_inc(stat, 1)
                    dve.wait_ge(stat, done + 2)
                    nc.vector.tensor_scalar(var[:], mv[:, :, 1], EPS, None, ALU.add).then_inc(var_ready, 1)
                if main:
                    dve.wait_ge(xnT_ready, c + 1)
                    if not (isinstance(c, int) and c < 1):
                        dve.wait_ge(y8_ready, c)
                    nc.vector.tensor_scalar(quant[:], xnT[:, k], scales[:, 2:3], FP8_MAX, ALU.mult,
                                            ALU.min).then_inc(quant_chain, 1)
                    dve.wait_ge(quant_chain, 3 * c + 1)
                    nc.vector.tensor_scalar(quant[:], quant[:], -FP8_MAX, None, ALU.max).then_inc(quant_chain, 1)
                    dve.wait_ge(quant_chain, 3 * c + 2)
                    nc.vector.tensor_scalar(power[:].bitcast(I32), quant[:].bitcast(I32), 0x7F800000, None,
                                            ALU.bitwise_and).then_inc(quant_chain, 1)
                    dve.wait_ge(quant_chain, 3 * c + 3)
                    nc.vector.tensor_scalar(power[:], power[:], FP8_MIN_NORMAL, ROUND, ALU.max,
                                            ALU.mult).then_inc(power_ready, 1)
                if ahead:
                    dve.wait_ge(dev_ready, c + 2)
                    nc.vector.reciprocal(newton[:, 0], dev[:]).then_inc(stat, 1)
                    dve.wait_ge(stat, done + 3)
                    nc.vector.tensor_tensor(newton[:, 1], newton[:, 0], newton[:, 0], ALU.mult).then_inc(stat, 1)
                    dve.wait_ge(stat, done + 4)
                    nc.vector.tensor_tensor(newton[:, 2], newton[:, 1], var[:], ALU.mult).then_inc(stat, 1)
                    dve.wait_ge(stat, done + 5)
                    nc.vector.tensor_scalar(newton[:, 1], newton[:, 2], -0.5, 1.5, ALU.mult, ALU.add).then_inc(stat, 1)
                    dve.wait_ge(stat, done + 6)
                    nc.vector.tensor_tensor(rstd[:], newton[:, 1], newton[:, 0], ALU.mult).then_inc(setup, 1)
                    dve.wait_ge(setup, c + 6)
                    for t in range(TT):
                        last = nc.vector.tensor_scalar(xn[:, k1, t], x_in[:, k1, t], mv[:, t, 0:1],
                                                       rstd[:, t:t + 1], ALU.subtract, ALU.mult)
                    last.then_inc(xn_ready, 1)
                if main:
                    for w, src in ((0, ps_q), (1, ps_k)):
                        dve.wait_ge(hi_ready, 2 * c + w + 1)
                        nc.vector.tensor_tensor(rest[:, w], src, qk_parts[:, k, w, 0],
                                                ALU.subtract).then_inc(rest_ready, 1)
                    for w in range(2):
                        dve.wait_ge(mid_ready, 2 * c + w + 1)
                        nc.vector.tensor_tensor(qk_parts[:, k, w, 2], rest[:, w], qk_parts[:, k, w, 1],
                                                ALU.subtract).then_inc(lo_ready, 1)
                    dve.wait_ge(f_ready, c + 1)
                    dve.wait_ge(xb_ready, c + 1)
                    if not (isinstance(c, int) and c < 2):
                        dve.wait_ge(base_stored[k], 16 * half(j, n))
                    nc.vector.tensor_tensor(base[:, k].rearrange("p t f -> p (t f)"),
                                            ps_f.rearrange("p a f -> p (a f)"),
                                            xb[:].rearrange("p t f -> p (t f)"), ALU.add).then_inc(base_ready, 1)

            chunks(dve, body)

        @block.tensor
        def _(pe):
            pe.wait_ge(c_loaded, 16 * 10)

            def body(j, n):
                c = CPB * j + n
                k, k1 = n % 2, (n + 1) % 2
                main = not (isinstance(c, int) and c < 0)
                ahead = not (isinstance(c, int) and c + 1 > B * CPB - 1)
                if main:
                    if isinstance(c, int) and c == 0:
                        pe.wait_ge(w_loaded, 48)
                    pe.wait_ge(xnT_ready, c + 1)
                    if not (isinstance(c, int) and c < 1):
                        pe.wait_ge(rest_ready, 2 * c - 1)
                    for m in range(KC):
                        for i in range(KC):
                            last = nc.tensor.matmul(ps_q[:, m], wq[:, i, m * P:(m + 1) * P], xnT[:, k, i],
                                                    start=(i == 0), stop=(i == KC - 1))
                    last.then_inc(q_ready, 1)
                if ahead:
                    pe.wait_ge(xn_ready, c + 2)
                    if not (isinstance(c, int) and c < 1):
                        pe.wait_ge(base_ready, c)
                    for i in range(KC):
                        for t in range(TT):
                            last = nc.tensor.transpose(ps_t[:, i, t * P:(t + 1) * P],
                                                       xn[:, k1, t, i * P:(i + 1) * P], keep["ident"][:])
                    last.then_inc(t_ready, 1)
                if main:
                    if not (isinstance(c, int) and c < 1):
                        pe.wait_ge(rest_ready, 2 * c)
                    grouped = xnT[:, k].rearrange("p i (g r) -> p i g r", r=STRIDE)
                    ns = CH // STRIDE
                    for m in range(KC):
                        for cols, keys in ((slice(0, ns), grouped[:, :, :, 0]), (slice(ns, CH), grouped[:, :, :, 1:])):
                            for i in range(KC):
                                last = nc.tensor.matmul(ps_k[:, m, cols], wk[:, i, m * P:(m + 1) * P], keys[:, i],
                                                        start=(i == 0), stop=(i == KC - 1))
                    last.then_inc(k_ready, 1)
                    if not (isinstance(c, int) and c < 1):
                        pe.wait_ge(v_copied, c)
                    for t in range(TT):
                        for i in range(KC):
                            last = nc.tensor.matmul(ps_v[:, t // 2, t % 2 * H:(t % 2 + 1) * H],
                                                    xnT[:, k, i, t * P:(t + 1) * P], wv[:, i],
                                                    start=(i == 0), stop=(i == KC - 1))
                    last.then_inc(v_ready, 1)
                    if isinstance(c, int) and c == 0:
                        pe.wait_ge(w8_ready, 1)
                    pe.wait_ge(y8_ready, c + 1)
                    if ahead:
                        pe.wait_ge(xnT_ready, c + 2)
                    else:
                        pe.wait_ge(base_ready, c)
                    for t in range(TT):
                        for i in range(KC):
                            for part in range(PARTS):
                                last = nc.tensor.matmul(ps_f[:, t // 2, t % 2 * H:(t % 2 + 1) * H],
                                                        y8[:, k, i, t * P:(t + 1) * P], w8_parts[:, part, i],
                                                        start=(i == 0 and part == 0),
                                                        stop=(i == KC - 1 and part == PARTS - 1))
                    last.then_inc(f_ready, 1)

            chunks(pe, body)


ROUNDS = NS // P + 1
SU = ROUNDS * HG
T_AT, M_AT = 3, 1
FIRST, LAST = -2, STEPS + 1


def v_units(s):
    units = []
    for r in range(ROUNDS):
        if r == M_AT and -1 <= s and s + 1 < STEPS:
            units.append(("negmax",))
        if r == T_AT and 1 <= s <= STEPS:
            units.append(("out",))
        if s + 2 < STEPS:
            units += [("max", r * HG + h) for h in range(HG)]
    return units


def part_attend(nc, dram, keep):
    before = {FIRST: 0}
    for s in range(FIRST, LAST + 1):
        before[s + 1] = before[s] + len(v_units(s))

    class Step:

        def __init__(self, j, n):
            self.j, self.n = j, n

        def at(self, d=0):
            return 2 * CPB * self.j + self.n + d

        def exists(self, d=0):
            return not isinstance(self.at(d), int) or 0 <= self.at(d) < STEPS

        def queries(self, d=0):
            return (self.n + d) % CPB

        def iteration(self, d=0):
            return 2 * self.j + (self.n + d) // CPB

        def parity(self, d=0):
            return (self.n + d) // CPB % 2

        def half_iteration(self, d=0):
            return self.j + (self.n + d) // CPB // 2

        def half(self, d=0):
            return CPB * self.j + (self.n + d) // 2

        def units(self):
            return v_units(self.n)

        def unit(self, d, i):
            return 2 * CPB * len(v_units(2)) * self.j + before[self.n + d] + i + 1

        def unit_named(self, d, kind):
            return self.unit(d, v_units(self.n + d).index(kind))

        def bank_free(self, i):
            if i >= 3:
                return self.unit(0, i - 3)
            if self.n - 1 not in before or not v_units(self.n - 1):
                return None
            count = len(v_units(self.n - 1))
            return self.unit(-1, max(u for u in range(count) if u % 3 == i))

    def steps(eng, body):
        for n in range(FIRST, 2):
            body(Step(0, n))
        with eng.Fori(0, (STEPS - 8) // 8) as j:
            for n in range(2, 10):
                body(Step(j, n))
        for n in range(STEPS - 6, LAST + 1):
            body(Step(0, n))

    with ExitStack() as ctx:
        def sb(name, shape, dt=F32):
            return ctx.enter_context(nc.sbuf_tensor(name, shape, dt))

        def sem(name):
            return ctx.enter_context(nc.semaphore(name))

        ps = ctx.enter_context(nc.psum_tensor("ps_attend", [P, 8, CH], F32))
        ps_s = [ps[:, i] for i in range(3)]
        ps_v = [ps[:, 3 + i] for i in range(3)]
        ps_o = [ps[:, 6 + i] for i in range(2)]

        q_op = [sb(f"q_op{i}", [P, HG * S], BF16) for i in range(2)]
        k_op = [sb(f"k_op{i}", [P, HG * S + 2 * WPAD], BF16) for i in range(2)]
        v_op = [sb(f"v_op{i}", [P, NS // P + S // P, HG * VW]) for i in range(2)]
        probs = sb("probs", [P, ROUNDS, HG, CH])
        out_rows = sb("out_rows", [P, 2, CH])
        peak = sb("peak", [P, 2, HG, TT])
        top = sb("top", [P, HG, TT])
        top_rest = sb("top_rest", [P, HG, TT])
        negmax = sb("negmax", [P, 2, HG, PARTS, TT], BF16)
        negmax_rows = sb("negmax_rows", [P, 2, P], BF16)
        rden = sb("rden", [P, 2, TT * HG])
        attn = sb("attn", [P, 2, TT * HG, D])
        scale = sb("scale", [P, 2])

        tails_set = sem("tails_set")
        ones_set = sem("ones_set")
        scale_ready = sem("scale_ready")
        qk_loaded = [sem(f"qk_loaded{i}") for i in range(2)]
        v_loaded = [sem(f"v_loaded{i}") for i in range(2)]
        s_ready = sem("s_ready")
        exp_done = sem("exp_done")
        pv_done = sem("pv_done")
        out_copied = sem("out_copied")
        u_ready = sem("u_ready")
        u_used = sem("u_used")
        top_chain = sem("top_chain")
        negmax_ready = sem("negmax_ready")
        negmax_stored = sem("negmax_stored")
        negmax_loaded = sem("negmax_loaded")
        rden_ready = sem("rden_ready")
        attn_stored = [sem(f"attn_stored{i}") for i in range(2)]

        block = ctx.enter_context(nc.Block())

        def window(tile):
            return NS - WPAD + WSTEP * tile

        @block.gpsimd
        def _(pool):
            for par in range(2):
                nc.gpsimd.memset(k_op[par][:, HG * S:], 0.0).then_inc(tails_set, 1)
                pool.wait_ge(tails_set, par + 1)
            for par in range(2):
                nc.gpsimd.memset(k_op[par][KR:KM, 0:HG * S], 1.0).then_inc(ones_set, 1)
                pool.wait_ge(ones_set, par + 1)

        @block.sync
        def _(sp):
            def body(st):
                if ("negmax",) in st.units():
                    par, cols = st.n % 2, slice(st.queries(1) * CH, (st.queries(1) + 1) * CH)
                    sp.wait_ge(u_used, st.unit_named(0, ("negmax",)))
                    if st.n >= 1:
                        sp.wait_ge(negmax_loaded, 16 * st.at(0))
                    sp.dma_start(dram["negmax"][par].rearrange("k (t q) -> (k t) q", q=P),
                                   negmax_rows[0:HG * PARTS * TT, par]).then_inc(negmax_stored, 16)
                    sp.wait_ge(negmax_stored, 16 * st.at(2))
                    sp.dma_start(
                        q_op[st.parity(1)][KR:KM, :].rearrange("p (h s) -> p h s", h=HG)[:, :, cols],
                        dram["negmax"][par].rearrange("(h a) s -> a h s", a=PARTS)).then_inc(negmax_loaded, 16)
                if ("out",) in st.units():
                    sp.wait_ge(u_used, st.unit_named(0, ("out",)))
                    rows = slice(st.queries(-1) * CH, (st.queries(-1) + 1) * CH)
                    sp.dma_start(
                        dram["attn"][st.iteration(-1), rows, :].rearrange("(t p) w -> p t w", p=P),
                        attn[:, (st.n - 1) % 2].rearrange("p (t h) d -> p t (h d)", t=TT)).then_inc(attn_stored[(st.n - 1) % 2], 16)

            steps(sp, body)
            for k in range(2):
                sp.wait_ge(attn_stored[k], 16 * STEPS // 2)

        @block.scalar
        def _(act):
            def load(it, par):
                q, k, v = dram["qk"][0], dram["qk"][1], dram["v"]

                def rows(t, a, b):
                    return t[it, a:b].rearrange("a (r h) s -> (a r) (h s)", h=HG)

                act.dma_start(k_op[par][0:3 * D, 0:HG * S], rows(k, 0, 3)).then_inc(qk_loaded[par], 16)
                act.dma_start(k_op[par][3 * D:5 * D, 0:HG * S], rows(k, 0, 2)).then_inc(qk_loaded[par], 16)
                act.dma_start(k_op[par][5 * D:6 * D, 0:HG * S], rows(k, 0, 1)).then_inc(qk_loaded[par], 16)
                act.dma_start(q_op[par][0:3 * D, :], rows(q, 0, 1).partition_broadcast(3)).then_inc(qk_loaded[par], 16)
                act.dma_start(q_op[par][3 * D:5 * D, :], rows(q, 1, 2).partition_broadcast(2)).then_inc(qk_loaded[par], 16)
                act.dma_start(q_op[par][5 * D:6 * D, :], rows(q, 2, 3)).then_inc(qk_loaded[par], 16)
                act.dma_start(v_op[par][:, 0:NS // P, :],
                             v[it, LOCAL:LOCAL + S, :].rearrange("(c p r) w -> r p c w", p=P, r=STRIDE)[0]
                             ).then_inc(v_loaded[par], 16)
                for r in range(STRIDE - 1):
                    one = v[it]
                    src = bass.AP(tensor=one.tensor, offset=one.offset + (1 + r) * HG * VW,
                                  ap=[[STRIDE * HG * VW, WIN // 3], [P * HG * VW, S // P], [1, HG * VW]])
                    act.dma_start(v_op[par][r:WIN:STRIDE - 1, NS // P:, :], src).then_inc(v_loaded[par], 16)

            load(0, 0)
            nc.scalar.activation(scale[:, 0:1], keep["unity"][:], ACT.Tanh, scale=0.5).then_inc(scale_ready, 1)
            act.wait_ge(scale_ready, 2)

            def copy_out(st):
                act.wait_ge(pv_done, ROUNDS * st.at())
                if st.n >= 3:
                    act.wait_ge(u_ready, st.unit_named(-2, ("out",)))
                nc.scalar.activation(out_rows[:, (st.n - 1) % 2], ps_o[(st.n - 1) % 2], ACT.Copy).then_inc(out_copied, 1)

            def body(st):
                for r in range(ROUNDS):
                    for h in range(HG):
                        if st.exists():
                            i = r * HG + h
                            act.wait_ge(s_ready, SU * st.at() + i + 1)
                            if h == 0 and st.n >= 1:
                                act.wait_ge(pv_done, ROUNDS * st.at(-1) + r + 1)
                            rows = P if r < ROUNDS - 1 else WIN
                            nc.scalar.activation(probs[0:rows, r, h], ps_s[i % 3][0:rows], ACT.Exp,
                                                 scale=scale[0:rows, 1:2]).then_inc(exp_done, 1)
                        if r == 2 and h == 1 and st.exists(-1):
                            copy_out(st)
                        if r == 2 and h == 1 and st.queries() == 0 and st.exists() and st.exists(4):
                            load(st.iteration(4), st.parity(4))

            steps(act, body)

        @block.vector
        def _(dve):
            dve.wait_ge(scale_ready, 1)
            nc.vector.tensor_scalar(scale[:, 1:2], scale[:, 0:1], 0.5 * D ** -0.5, 0.5 * D ** -0.5, ALU.mult,
                                    ALU.add).then_inc(scale_ready, 1)

            def body(st):
                units = st.units()
                for i, unit in enumerate(units):
                    src = ps_v[i % 3]
                    dve.wait_ge(u_ready, st.unit(0, i))
                    if unit[0] == "max":
                        m = unit[1]
                        h = m % HG
                        if m < TT * HG:
                            ins = nc.vector.tensor_reduce(peak[:, 0, h, m // HG:m // HG + 1], src, AX_X, ALU.max)
                        else:
                            ins = nc.vector.tensor_reduce(
                                peak[:, 1, h], src[:, 0:TT * WIN].rearrange("p (t w) -> p t w", t=TT), AX_X, ALU.max)
                    elif unit[0] == "negmax":
                        par = st.n % 2
                        if st.n >= 1:
                            dve.wait_ge(negmax_stored, 16 * st.at())
                        ins = nc.vector.tensor_copy(negmax_rows[0:HG * PARTS * TT, par],
                                                    src[0:HG * PARTS * TT, 0:P])
                    else:
                        out = src.rearrange("p (u w) -> p u w", w=VW)
                        nc.vector.reciprocal(rden[:, st.n % 2], out[:, :, D]).then_inc(rden_ready, 1)
                        dve.wait_ge(rden_ready, st.at())
                        if st.n >= 3:
                            dve.wait_ge(attn_stored[(st.n - 1) % 2], 16 * st.half(-1))
                        ins = nc.vector.tensor_tensor(attn[:, (st.n - 1) % 2], out[:, :, 0:D],
                                                      rden[:, st.n % 2].unsqueeze(2).broadcast_to([P, TT * HG, D]), ALU.mult)
                    ins.then_inc(u_used, 1)
                if st.exists(2):
                    dve.wait_ge(u_used, st.unit(0, len(units) - 1))
                    done = 4 * st.at(2)
                    parts = negmax[:, st.n % 2]
                    nc.vector.tensor_tensor(top[:], peak[:, 0], peak[:, 1], ALU.max).then_inc(top_chain, 1)
                    dve.wait_ge(top_chain, done + 1)
                    nc.vector.tensor_scalar(parts[:, :, 0], top[:], -1.0, None, ALU.mult).then_inc(top_chain, 1)
                    dve.wait_ge(top_chain, done + 2)
                    nc.vector.scalar_tensor_tensor(top_rest[:], top[:], -1.0, parts[:, :, 0], ALU.mult,
                                                   ALU.subtract).then_inc(top_chain, 1)
                    dve.wait_ge(top_chain, done + 3)
                    nc.vector.tensor_copy(parts[:, :, 1], top_rest[:]).then_inc(top_chain, 1)
                    dve.wait_ge(top_chain, done + 4)
                    nc.vector.tensor_tensor(parts[:, :, 2], top_rest[:], parts[:, :, 1],
                                            ALU.subtract).then_inc(negmax_ready, 1)

            steps(dve, body)

        @block.tensor
        def _(pe):
            def score(st, r, h):
                i = r * HG + h
                q, k, q0 = q_op[st.parity()], k_op[st.parity()], h * S + st.queries() * CH
                if i == 0:
                    pe.wait_ge(negmax_loaded, 16 * st.at(1))
                    if st.n == 0:
                        pe.wait_ge(ones_set, 2)
                if i >= 3:
                    pe.wait_ge(exp_done, SU * st.at() + i - 2)
                elif st.n >= 1:
                    pe.wait_ge(exp_done, SU * st.at(-1) + {0: 19, 1: 20, 2: 18}[i])
                if r < ROUNDS - 1:
                    ins = nc.tensor.matmul(ps_s[i % 3], k[0:KM, h * S + r * P:h * S + (r + 1) * P],
                                           q[0:KM, q0:q0 + CH], start=True, stop=True)
                else:
                    mask = {0: 0, CPB - 1: 2}.get(st.queries(), 1)
                    nc.tensor.matmul(ps_s[i % 3][0:WIN], keep["ident_bf"][0:WIN, 0:WIN], keep["key_mask"][0:WIN, mask],
                                     start=True, stop=False)
                    for t in range(TT):
                        at = h * S + window(st.queries() * TT + t)
                        ins = nc.tensor.matmul(ps_s[i % 3][0:WIN, t * P:(t + 1) * P], k[0:KM, at:at + WIN],
                                               q[0:KM, q0 + t * P:q0 + (t + 1) * P], start=False, stop=(t == TT - 1))
                ins.then_inc(s_ready, 1)

            def unit(st, i, kind, m):
                bank = ps_v[i % 3]
                free = st.bank_free(i)
                if free is not None:
                    pe.wait_ge(u_used, free)
                if kind == "max":
                    q, k = q_op[st.parity(2)], k_op[st.parity(2)]
                    t, h = m // HG, m % HG
                    q0 = h * S + st.queries(2) * CH
                    if m == 0 and st.queries(2) == 0:
                        pe.wait_ge(qk_loaded[st.parity(2)], 96 * (st.half_iteration(2) + 1))
                    if t < TT:
                        ins = nc.tensor.matmul(bank, q[0:KR, q0 + t * P:q0 + (t + 1) * P],
                                               k[0:KR, h * S:h * S + NS], start=True, stop=True)
                    else:
                        mask = {0: 0, CPB - 1: 2}.get(st.queries(2), 1)
                        nc.tensor.matmul(bank[:, 0:TT * WIN], keep["ident_bf"][:], keep["max_mask"][:, mask],
                                         start=True, stop=False)
                        for t in range(TT):
                            at = h * S + window(st.queries(2) * TT + t)
                            ins = nc.tensor.matmul(bank[:, t * WIN:(t + 1) * WIN], q[0:KR, q0 + t * P:q0 + (t + 1) * P],
                                                   k[0:KR, at:at + WIN], start=False, stop=(t == TT - 1))
                elif kind == "negmax":
                    pe.wait_ge(negmax_ready, st.at(2))
                    parts = negmax[:, (st.n + 1) % 2].rearrange("p h a t -> p (h a t)")
                    ins = nc.tensor.matmul(bank[0:HG * PARTS * TT, 0:P], parts, keep["ident_bf"][:],
                                           start=True, stop=True)
                else:
                    pe.wait_ge(out_copied, st.at())
                    for t in range(TT):
                        ins = nc.tensor.transpose(bank[:, t * P:(t + 1) * P],
                                                  out_rows[:, (st.n - 1) % 2, t * P:(t + 1) * P], keep["ident"][:])
                ins.then_inc(u_ready, 1)

            def weigh(st, d, r):
                out, v = ps_o[(st.n + d) % 2], v_op[st.parity(d)]
                if r == 0:
                    if st.queries(d) == 0:
                        pe.wait_ge(v_loaded[st.parity(d)], 64 * (st.half_iteration(d) + 1))
                    if st.n + d >= 2:
                        pe.wait_ge(out_copied, st.at(d - 1))
                if r < ROUNDS - 1:
                    pe.wait_ge(exp_done, SU * st.at(d) + (r + 1) * HG)
                    for h in range(HG):
                        ins = nc.tensor.matmul(out[h * VW:(h + 1) * VW], v[:, r, h * VW:(h + 1) * VW], probs[:, r, h],
                                               start=(r == 0), stop=False)
                else:
                    pe.wait_ge(exp_done, SU * st.at(d + 1))
                    for t in range(TT):
                        tile = NS // P + st.queries(d) * TT + t
                        for h in range(HG):
                            ins = nc.tensor.matmul(out[h * VW:(h + 1) * VW, t * P:(t + 1) * P],
                                                   v[0:WIN, tile, h * VW:(h + 1) * VW],
                                                   probs[0:WIN, r, h, t * P:(t + 1) * P],
                                                   start=False, stop=(t == TT - 1))
                ins.then_inc(pv_done, 1)

            def body(st):
                units = list(enumerate(st.units()))

                def next_unit():
                    i, u = units.pop(0)
                    unit(st, i, u[0], u[-1])

                for r in range(ROUNDS):
                    while units and units[0][1][0] != "max" and (
                            r >= (M_AT if units[0][1][0] == "negmax" else T_AT)):
                        next_unit()
                    for h in range(HG):
                        if st.exists():
                            score(st, r, h)
                        if units and units[0][1][0] == "max":
                            next_unit()
                    if r >= 2 and st.exists():
                        weigh(st, 0, r - 2)
                    if r < 2 and st.exists(-1):
                        weigh(st, -1, r + 3)

            pe.wait_ge(tails_set, 2)
            steps(pe, body)


def part_finish(nc, io, dram, keep, out):
    with ExitStack() as ctx:
        def sb(name, shape, dt=F32):
            return ctx.enter_context(nc.sbuf_tensor(name, shape, dt))

        def sem(name):
            return ctx.enter_context(nc.semaphore(name))

        ps = ctx.enter_context(nc.psum_tensor("ps_finish", [P, 8, CH], F32))
        ps_t = [ps[:, 2 * i:2 * i + 2] for i in range(2)]
        ps_y = [ps[:, 4 + 2 * i:6 + 2 * i] for i in range(2)]
        heads = sb("heads", [P, 2, TT, H])
        heads_T = sb("heads_T", [P, 2, KC, CH])
        base = sb("base_in", [P, 2, TT, H])
        total = sb("total", [P, 2, TT, H])
        heads_loaded = [sem(f"heads_loaded{i}") for i in range(2)]
        base_loaded = [sem(f"base_loaded{i}") for i in range(2)]
        turned = sem("turned")
        copied = sem("copied")
        y_ready = sem("y_ready")
        total_ready = sem("total_ready")
        out_stored = [sem(f"out_stored{i}") for i in range(2)]
        base_rows = dram["base"].rearrange("(c t p) f -> c p t f", t=TT, p=P)
        out_rows = out.rearrange("b (c t p) f -> (b c) p t f", t=TT, p=P)
        block = ctx.enter_context(nc.Block())

        def chunks(eng, body):
            for n in range(CPB):
                body(0, n)
            with eng.Fori(1, B) as j:
                for n in range(CPB):
                    body(j, n)

        @block.sync
        def _(sp):
            def body(j, n):
                c, k = CPB * j + n, n % 2
                early = isinstance(c, int) and c < 2
                if not early:
                    sp.wait_ge(turned, c - 1)
                for t in range(TT):
                    row = n * CH + t * P
                    sp.dma_start(heads[:, k, t].rearrange("p (g w) -> p g w", g=G),
                                 dram["attn"][bass.ds(j * G, G), row:row + P, :].rearrange("g p w -> p g w")
                                 ).then_inc(heads_loaded[k], 16)
                if not early:
                    sp.wait_ge(total_ready, c - 1)
                sp.dma_start(base[:, k], base_rows[c]).then_inc(base_loaded[k], 16)

            chunks(sp, body)

        @block.tensor
        def _(pe):
            def body(j, n):
                c, k = CPB * j + n, n % 2
                early = isinstance(c, int) and c < 2
                pe.wait_ge(heads_loaded[k], 16 * TT * (CPB // 2 * j + n // 2 + 1))
                if not early:
                    pe.wait_ge(copied, c - 1)
                for i in range(KC):
                    for t in range(TT):
                        last = nc.tensor.transpose(ps_t[k][:, i, t * P:(t + 1) * P],
                                                   heads[:, k, t, i * P:(i + 1) * P], keep["ident"][:])
                last.then_inc(turned, 1)
                pe.wait_ge(copied, c + 1)
                if not early:
                    pe.wait_ge(total_ready, c - 1)
                for t in range(TT):
                    for i in range(KC):
                        last = nc.tensor.matmul(ps_y[k][:, t // 2, t % 2 * H:(t % 2 + 1) * H],
                                                heads_T[:, k, i, t * P:(t + 1) * P], keep["wo"][:, i],
                                                start=(i == 0), stop=(i == KC - 1))
                last.then_inc(y_ready, 1)

            chunks(pe, body)

        @block.scalar
        def _(act):
            def body(j, n):
                c, k = CPB * j + n, n % 2
                act.wait_ge(turned, c + 1)
                if not (isinstance(c, int) and c < 2):
                    act.wait_ge(y_ready, c - 1)
                nc.scalar.activation(heads_T[:, k], ps_t[k], ACT.Copy).then_inc(copied, 1)
                act.wait_ge(total_ready, c + 1)
                act.dma_start(out_rows[c], total[:, k]).then_inc(out_stored[k], 16)

            chunks(act, body)
            for k in range(2):
                act.wait_ge(out_stored[k], 16 * B * CPB // 2)

        @block.vector
        def _(dve):
            def body(j, n):
                c, k = CPB * j + n, n % 2
                dve.wait_ge(y_ready, c + 1)
                dve.wait_ge(base_loaded[k], 16 * (CPB // 2 * j + n // 2 + 1))
                if not (isinstance(c, int) and c < 2):
                    dve.wait_ge(out_stored[k], 16 * (CPB // 2 * j + n // 2))
                nc.vector.tensor_tensor(total[:, k].rearrange("p t f -> p (t f)"),
                                        ps_y[k].rearrange("p a f -> p (a f)"),
                                        base[:, k].rearrange("p t f -> p (t f)"), ALU.add).then_inc(total_ready, 1)

            chunks(dve, body)


def build(nc, io, out):
    dram = {
        "qk": [nc.dram_tensor(f"{n}_parts_dram", [NIT, PARTS, HG * D, S], BF16).ap() for n in "qk"],
        "v": nc.dram_tensor("v_dram", [NIT, LOCAL + S + LOCAL, HG * VW], F32).ap(),
        "base": nc.dram_tensor("base_dram", [B * S, H], F32).ap(),
        "attn": nc.dram_tensor("attn_dram", [NIT, S, HG * D], F32).ap(),
        "negmax": nc.dram_tensor("negmax_dram", [2, HG * PARTS, CH], BF16).ap(),
    }
    with ExitStack() as ctx:
        def sb(name, shape, dt=F32):
            return ctx.enter_context(nc.sbuf_tensor(name, shape, dt))

        keep = {
            "ident": sb("ident", [P, P]),
            "ident_bf": sb("ident_bf", [P, P], BF16),
            "max_mask_f": sb("max_mask_f", [P, MASKS, TT * WIN]),
            "max_mask": sb("max_mask", [P, MASKS, TT * WIN], BF16),
            "key_mask_f": sb("key_mask_f", [P, MASKS, CH]),
            "key_mask": sb("key_mask", [P, MASKS, CH], BF16),
            "wo": sb("wo", [P, KC, H]),
            "unity": sb("unity", [P, 1]),
        }
        part_project(nc, io, dram, keep)
        part_attend(nc, dram, keep)
        part_finish(nc, io, dram, keep, out)


def kernel(L0_attn_x, L0_attn_q_w, L0_attn_k_w, L0_attn_v_w, L0_attn_o_w, L0_attn_o_b, L0_attn_unity_scale,
           L0_ffn_weight_fp8, L0_ffn_bias, L0_ffn_input_scale, L0_ffn_weight_scale):
    import numpy as np
    import concourse.bacc as bacc
    from concourse.bass_utils import run_bass_kernel_spmd

    q = np.arange(P)
    key = np.arange(WIN)
    rel = STRIDE * (key // 3) + 1 + key % 3 - LOCAL
    near = np.abs(rel[:, None] - q[None, :]) <= LOCAL
    seen = np.stack([np.stack([near] * TT, 1)] * MASKS)
    seen[0, :, 0] &= (rel >= 0)[:, None]
    seen[MASKS - 1, :, TT - 1] &= (rel < P)[:, None]
    key_mask = np.where(seen, np.float32(0), np.float32(-BIG)).reshape(MASKS, WIN, CH)
    max_mask = np.where(seen.transpose(0, 3, 2, 1), np.float32(0), np.float32(-BIG)).reshape(MASKS, P, TT * WIN)

    def columns(w):
        w = np.asarray(w).reshape(H, KC, G // KC, HG, D)
        return np.ascontiguousarray(w.transpose(0, 1, 2, 4, 3)).reshape(H, H)

    arrays = {
        "x": np.asarray(L0_attn_x),
        "q_w": columns(L0_attn_q_w),
        "k_w": columns(L0_attn_k_w),
        "v_w": np.asarray(L0_attn_v_w),
        "o_w": np.asarray(L0_attn_o_w),
        "o_b": np.asarray(L0_attn_o_b),
        "unity": np.asarray(L0_attn_unity_scale).reshape(1),
        "w8T": np.ascontiguousarray(np.asarray(L0_ffn_weight_fp8).T),
        "ffn_bias": np.asarray(L0_ffn_bias),
        "input_scale": np.asarray(L0_ffn_input_scale),
        "weight_scale": np.asarray(L0_ffn_weight_scale),
        "ident": np.eye(P, dtype=np.float32),
        "max_mask": np.ascontiguousarray(max_mask),
        "key_mask": np.ascontiguousarray(key_mask),
    }
    nc = bacc.Bacc("TRN2", target_bir_lowering=False, num_devices=1)
    io = {n: nc.dram_tensor(f"in_{n}", a.shape, mybir.dt.from_np(a.dtype), kind="ExternalInput").ap()
          for n, a in arrays.items()}
    out = nc.dram_tensor("out", [B, S, H], F32, kind="ExternalOutput").ap()
    build(nc, io, out)
    r = run_bass_kernel_spmd(nc, [{f"in_{n}": a for n, a in arrays.items()}], core_ids=[0])
    return r.results[0]["out"]
```

```python
from contextlib import ExitStack

import concourse.bass as bass
from concourse import mybir

F32 = mybir.dt.float32
BF16 = mybir.dt.bfloat16
I32 = mybir.dt.int32
ALU = mybir.AluOpType
ACT = mybir.ActivationFunctionType
AX_X = mybir.AxisListType.X

B, S, H = 4, 2048, 256
NH, D = 16, 16
P = 128
KC = H // P
CH = 512
TT = CH // P
CPB = S // CH
G, HG = 4, 4
NIT = B * G
STEPS = NIT * CPB
STRIDE, LOCAL = 4, 8
NS = S // STRIDE
WIN = (P + 2 * LOCAL) // STRIDE * (STRIDE - 1)
WSTEP = P // STRIDE * (STRIDE - 1)
WPAD = LOCAL // STRIDE * (STRIDE - 1)
PARTS = 3
KR = 6 * D
KM = KR + PARTS
QK_LOADS = 2 * 6
VW = 2 * D
EPS = 1e-5
FP8_MAX = 448.0
FP8_MIN_NORMAL = 2.0 ** -6
ROUND = 1.5 * 2.0 ** 20
BIG = 1e30
MASKS = 3


def chunks(eng, body):
    for n in range(-1, 3):
        body(0, n)
    with eng.Fori(0, B - 2) as j:
        for n in range(3, 3 + CPB):
            body(j, n)
    for n in range(B * CPB - CPB - 1, B * CPB):
        body(0, n)


def load_qk(eng, dram, operands, it, par, which=("k_op", "q_op"), rows=range(6)):
    q, k = dram["qk"]

    for op, source, parts in (("k_op", k, (0, 1, 2, 0, 1, 0)), ("q_op", q, (0, 0, 0, 1, 1, 2))):
        for i in rows if op in which else ():
            part = parts[i]
            eng.dma_start(operands[op][i * D:(i + 1) * D, 0:HG * S],
                          source[part, it].rearrange("(r h) s -> r (h s)", h=HG)
                          ).then_inc(operands["qk_loaded"][par], 16)


def part_project(nc, io, dram, keep):
    with ExitStack() as ctx:
        def sb(name, shape, dt=F32):
            return ctx.enter_context(nc.sbuf_tensor(name, shape, dt))

        def sem(name):
            return ctx.enter_context(nc.semaphore(name))

        ps = ctx.enter_context(nc.psum_tensor("ps_project", [P, 8, CH], F32))
        ps_q, ps_t, ps_k, ps_v = (ps[:, 2 * i:2 * i + 2, :] for i in range(4))
        ps_f = ps_t

        wq, wk, wv = (sb(n, [P, KC, H]) for n in ("wq", "wk", "wv"))
        w8 = sb("w8", [P, KC, H])
        w8_rest = sb("w8_rest", [P, KC, H])
        w8_parts = sb("w8_parts", [P, PARTS, KC, H], BF16)
        bias = sb("bias", [P, H])
        bias_o = sb("bias_o", [P, H])
        scales = sb("scales", [P, 3])
        x_in = sb("x_in", [P, 2, TT, H])
        stats = sb("stats", [P, TT, 6])
        counts = sb("counts", [P, TT])
        mv = sb("mv", [P, TT, 2])
        var = sb("var", [P, TT])
        dev = sb("dev", [P, TT])
        newton = sb("newton", [P, 3, TT])
        rstd = sb("rstd", [P, TT])
        xn = sb("xn", [P, 2, TT, H])
        key_mask_f = xn[:].rearrange("p k t f -> p (k t f)")[:, 0:MASKS * CH].rearrange(
            "p (m n) -> p m n", m=MASKS)
        xnT = sb("xnT", [P, 2, KC, CH])
        qk_parts = sb("qk_parts", [P, 2, 2, PARTS, KC, CH], BF16)
        rest = sb("rest", [P, 2, KC, CH])
        max_mask_f = rest[:].rearrange("p w i n -> p (w i n)")[:, 0:MASKS * TT * WIN].rearrange(
            "p (m n) -> p m n", m=MASKS)
        v_sb = sb("v_sb", [P, 2, TT, NH, VW])
        quant = sb("quant", [P, KC, CH])
        zeros = quant[0:NIT].rearrange("p i n -> p (i n)")[:, 0:LOCAL * HG * VW]
        power = sb("power", [P, KC, CH])
        y8 = sb("y8", [P, 2, KC, CH], BF16)

        w_loaded = sem("w_loaded")
        c_loaded = sem("c_loaded")
        zeros_set = sem("zeros_set")
        v_set = sem("v_set")
        pads_stored = sem("pads_stored")
        setup = sem("setup")
        w8_ready = sem("w8_ready")
        bias_ready = sem("bias_ready")
        x_loaded = [sem(f"x_loaded{i}") for i in range(2)]
        stat = sem("stat")
        var_ready = sem("var_ready")
        dev_ready = sem("dev_ready")
        xn_ready = sem("xn_ready")
        t_ready = sem("t_ready")
        xnT_ready = sem("xnT_ready")
        q_ready = sem("q_ready")
        k_ready = sem("k_ready")
        v_ready = sem("v_ready")
        f_ready = sem("f_ready")
        hi_ready = sem("hi_ready")
        rest_ready = sem("rest_ready")
        mid_ready = sem("mid_ready")
        lo_ready = sem("lo_ready")
        v_copied = sem("v_copied")
        quant_chain = sem("quant_chain")
        power_ready = sem("power_ready")
        sum_ready = sem("sum_ready")
        y8_ready = sem("y8_ready")
        xb_ready = sem("xb_ready")
        base_ready = sem("base_ready")
        qk_stored = [sem(f"qk_stored{i}") for i in range(2)]
        v_stored = [sem(f"v_stored{i}") for i in range(2)]

        x_rows = io["x"].rearrange("b (c t p) f -> (b c) p t f", t=TT, p=P)
        base = keep["base"].rearrange("p (c t) f -> p c (t f)", t=TT)
        block = ctx.enter_context(nc.Block())

        def half(j, n):
            return CPB // 2 * j + n // 2

        @block.sync
        def _(sp):
            sp.dma_start(keep["ident"][:], io["ident"]).then_inc(c_loaded, 16)
            sp.dma_start(x_in[:, 0], x_rows[0]).then_inc(x_loaded[0], 16)
            sp.dma_start(scales[:, 0:1], io["input_scale"].partition_broadcast(P)).then_inc(c_loaded, 16)
            sp.dma_start(scales[:, 1:2], io["weight_scale"].partition_broadcast(P)).then_inc(c_loaded, 16)
            sp.dma_start(w8[:], io["w8T"].rearrange("(k p) f -> p k f", p=P)).then_inc(c_loaded, 16)
            sp.dma_start(bias[:], io["ffn_bias"].partition_broadcast(P)).then_inc(c_loaded, 16)
            sp.dma_start(bias_o[:], io["o_b"].partition_broadcast(P)).then_inc(c_loaded, 16)
            for w, name in ((wq, "q_w"), (wk, "k_w"), (wv, "v_w")):
                sp.dma_start(w[:], io[name].rearrange("(k p) f -> p k f", p=P)).then_inc(w_loaded, 16)
            sp.dma_start(keep["unity"][:], io["unity"].partition_broadcast(P)).then_inc(c_loaded, 16)
            sp.dma_start(max_mask_f, io["max_mask"].rearrange("m p n -> p m n")).then_inc(c_loaded, 16)
            sp.dma_start(key_mask_f[0:WIN], io["key_mask"].rearrange("m p n -> p m n")).then_inc(c_loaded, 16)
            sp.dma_start(keep["wo"][:], io["o_w"].rearrange("(k p) f -> p k f", p=P)).then_inc(c_loaded, 16)
            sp.wait_ge(zeros_set, 1)
            for edge in (0, LOCAL + S):
                sp.dma_start(dram["v"][:, edge:edge + LOCAL, :].rearrange("i t w -> i (t w)"), zeros).then_inc(pads_stored, 16)

            def body(j, n):
                c = CPB * j + n
                if n == -1:
                    sp.dma_start(x_in[:, 1], x_rows[1]).then_inc(x_loaded[1], 16)
                if not (isinstance(c, int) and c + 3 > B * CPB - 1):
                    sp.wait_ge(xn_ready, c + 2)
                    sp.wait_ge(xb_ready, c + 2)
                    sp.dma_start(x_in[:, (n + 1) % 2], x_rows[c + 3]).then_inc(x_loaded[(n + 1) % 2], 16)
                if isinstance(c, int) and c < 0:
                    return
                b4, cq, k = (j + n // CPB) * G, n % CPB, n % 2
                pair = (j + n // CPB) * KC
                for w in range(2):
                    sp.wait_ge(lo_ready, 2 * c + w + 1)
                    ns = CH // STRIDE
                    spans = [(cq * ns, 0, ns), (NS + cq * (CH - ns), ns, CH)] if w else [(cq * CH, 0, CH)]
                    for part in range(PARTS):
                        pairs = dram["qk"][w][part].rearrange("(m u) r s -> m (u r) s", u=2)
                        for to, a, e in spans:
                            sp.dma_start(
                                pairs[bass.ds(pair, KC), :, to:to + e - a].rearrange("m r s -> r m s"),
                                qk_parts[:, k, w, part, :, a:e]).then_inc(qk_stored[k], 16)
                sp.wait_ge(v_copied, c + 1)
                for t in range(TT):
                    row = LOCAL + cq * CH + t * P
                    sp.dma_start(dram["v"][bass.ds(b4, G), row:row + P, :].rearrange("g p w -> p g w"),
                                 v_sb[:, k, t].rearrange("p (g h) w -> p g (h w)", g=G)).then_inc(v_stored[k], 16)
                if isinstance(c, int) and c == B * CPB - 2:
                    for par in range(2):
                        sp.wait_ge(qk_stored[par], 16 * 9 * (half(j, n) + 1 - par))
                    load_qk(sp, dram, keep, 0, 0)

            chunks(sp, body)
            sp.wait_ge(pads_stored, 32)
            for k in range(2):
                sp.wait_ge(qk_stored[k], 16 * 9 * B * CPB // 2)
                sp.wait_ge(v_stored[k], 16 * TT * B * CPB // 2)

        @block.gpsimd
        def _(pool):
            nc.gpsimd.memset(zeros, 0.0).then_inc(zeros_set, 1)
            nc.gpsimd.memset(v_sb[:, 0, :, :, D:VW], 1.0).then_inc(v_set, 1)
            nc.gpsimd.memset(v_sb[:, 1, :, :, D:VW], 1.0).then_inc(v_set, 1)
            pool.wait_ge(bias_ready, 1)

            def body(j, n):
                c = CPB * j + n
                k, k1 = n % 2, (n + 1) % 2
                if not (isinstance(c, int) and c + 1 > B * CPB - 1):
                    pool.wait_ge(x_loaded[k1], 16 * (half(j, n + 1) + 1))
                    nc.gpsimd.tensor_tensor(base[:, c + 1].rearrange("p (t f) -> p t f", t=TT), x_in[:, k1],
                                            bias[:].unsqueeze(1).broadcast_to([P, TT, H]),
                                            ALU.add).then_inc(xb_ready, 1)
                if isinstance(c, int) and c < 0:
                    return
                pool.wait_ge(power_ready, c + 1)
                nc.gpsimd.tensor_tensor(quant[:], quant[:], power[:], ALU.add).then_inc(sum_ready, 1)
                pool.wait_ge(sum_ready, c + 1)
                if not (isinstance(c, int) and c < 2):
                    pool.wait_ge(f_ready, c - 1)
                nc.gpsimd.tensor_tensor(y8[:, k], quant[:], power[:], ALU.subtract).then_inc(y8_ready, 1)

            chunks(pool, body)

        @block.scalar
        def _(act):
            def deviation(j, n, d):
                c = CPB * j + n + d
                if not (isinstance(c, int) and c > B * CPB - 1):
                    act.wait_ge(var_ready, c + 1)
                    nc.scalar.activation(dev[:], var[:], ACT.Sqrt).then_inc(dev_ready, 1)

            def body(j, n):
                c = CPB * j + n
                k = n % 2
                main = not (isinstance(c, int) and c < 0)
                ahead = not (isinstance(c, int) and c + 1 > B * CPB - 1)
                if main:
                    act.wait_ge(q_ready, c + 1)
                    if not (isinstance(c, int) and c < 2):
                        act.wait_ge(qk_stored[k], 16 * 9 * half(j, n))
                    nc.scalar.activation(qk_parts[:, k, 0, 0], ps_q, ACT.Copy).then_inc(hi_ready, 1)
                if ahead:
                    act.wait_ge(t_ready, c + 2)
                    if not (isinstance(c, int) and c < 1):
                        act.wait_ge(v_ready, c)
                        act.wait_ge(power_ready, c)
                    nc.scalar.activation(xnT[:, (n + 1) % 2], ps_t, ACT.Copy).then_inc(xnT_ready, 1)
                if main:
                    act.wait_ge(rest_ready, 2 * c + 1)
                    nc.scalar.activation(qk_parts[:, k, 0, 1], rest[:, 0], ACT.Copy).then_inc(mid_ready, 1)
                deviation(j, n, 2)
                if main:
                    act.wait_ge(k_ready, c + 1)
                    nc.scalar.activation(qk_parts[:, k, 1, 0], ps_k, ACT.Copy).then_inc(hi_ready, 1)
                    act.wait_ge(rest_ready, 2 * c + 2)
                    nc.scalar.activation(qk_parts[:, k, 1, 1], rest[:, 1], ACT.Copy).then_inc(mid_ready, 1)
                    act.wait_ge(v_ready, c + 1)
                    if isinstance(c, int) and c == 0:
                        act.wait_ge(v_set, 2)
                    if not (isinstance(c, int) and c < 2):
                        act.wait_ge(v_stored[k], 16 * TT * half(j, n))
                    nc.scalar.activation(
                        v_sb[:, k].rearrange("p t h w -> p (t h) w")[:, :, 0:D],
                        ps_v.rearrange("p a (t w) -> p (a t) w", w=D), ACT.Copy).then_inc(v_copied, 1)

            deviation(0, -1, 1)
            chunks(act, body)

        @block.vector
        def _(dve):
            dve.wait_ge(c_loaded, 16 * 10)
            nc.vector.tensor_copy(keep["max_mask"][:], max_mask_f)
            nc.vector.tensor_copy(keep["key_mask"][0:WIN], key_mask_f[0:WIN])
            nc.vector.tensor_copy(keep["ident_bf"][:], keep["ident"][:])
            nc.vector.reciprocal(scales[:, 2:3], scales[:, 0:1])
            nc.vector.tensor_tensor(bias[:], bias[:], bias_o[:], ALU.add).then_inc(bias_ready, 1)
            nc.vector.tensor_scalar(w8[:], w8[:], scales[:, 1:2], scales[:, 0:1], ALU.mult, ALU.mult).then_inc(setup, 1)
            dve.wait_ge(setup, 1)
            nc.vector.tensor_copy(w8_parts[:, 0], w8[:]).then_inc(setup, 1)
            dve.wait_ge(setup, 2)
            nc.vector.tensor_tensor(w8_rest[:], w8[:], w8_parts[:, 0], ALU.subtract).then_inc(setup, 1)
            dve.wait_ge(setup, 3)
            nc.vector.tensor_copy(w8_parts[:, 1], w8_rest[:]).then_inc(setup, 1)
            dve.wait_ge(setup, 4)
            nc.vector.tensor_tensor(w8_parts[:, 2], w8_rest[:], w8_parts[:, 1], ALU.subtract).then_inc(w8_ready, 1)

            def add_linear(c):
                dve.wait_ge(f_ready, c + 1)
                dve.wait_ge(xb_ready, c + 1)
                nc.vector.tensor_tensor(base[:, c], ps_f.rearrange("p a f -> p (a f)"), base[:, c],
                                        ALU.add).then_inc(base_ready, 1)

            def layernorm(j, n):
                c, k = CPB * j + n, n % 2
                if isinstance(c, int) and c > B * CPB - 1:
                    return
                done = 7 * c
                dve.wait_ge(x_loaded[k], 16 * (half(j, n) + 1))
                for t in range(TT):
                    last = nc.vector.bn_stats(stats[:, t], x_in[:, k, t])
                last.then_inc(stat, 1)
                dve.wait_ge(stat, done + 1)
                nc.vector.tensor_copy(counts[:], stats[:, :, 0])
                for t in range(TT):
                    last = nc.vector.bn_aggr(mv[:, t], stats[:, t])
                last.then_inc(stat, 1)
                dve.wait_ge(stat, done + 2)
                nc.vector.tensor_scalar(var[:], mv[:, :, 1], EPS, None, ALU.add).then_inc(var_ready, 1)
                dve.wait_ge(dev_ready, c + 1)
                nc.vector.reciprocal(newton[:, 0], dev[:]).then_inc(stat, 1)
                dve.wait_ge(stat, done + 3)
                nc.vector.tensor_tensor(newton[:, 1], newton[:, 0], newton[:, 0], ALU.mult).then_inc(stat, 1)
                dve.wait_ge(stat, done + 4)
                nc.vector.tensor_tensor(newton[:, 2], newton[:, 1], var[:], ALU.mult).then_inc(stat, 1)
                dve.wait_ge(stat, done + 5)
                nc.vector.tensor_scalar(newton[:, 1], newton[:, 2], -0.5, 1.5, ALU.mult, ALU.add).then_inc(stat, 1)
                dve.wait_ge(stat, done + 6)
                nc.vector.tensor_tensor(rstd[:], newton[:, 1], newton[:, 0], ALU.mult).then_inc(stat, 1)
                dve.wait_ge(stat, done + 7)
                if not (isinstance(c, int) and c < 2):
                    dve.wait_ge(t_ready, c - 1)
                for t in range(TT):
                    last = nc.vector.tensor_scalar(xn[:, k, t], x_in[:, k, t], mv[:, t, 0:1],
                                                   rstd[:, t:t + 1], ALU.subtract, ALU.mult)
                last.then_inc(xn_ready, 1)

            def cut(c, k, w):
                src = (ps_q, ps_k)[w]
                dve.wait_ge(hi_ready, 2 * c + w + 1)
                nc.vector.tensor_tensor(rest[:, w], src, qk_parts[:, k, w, 0], ALU.subtract).then_inc(rest_ready, 1)

            def body(j, n):
                c, k = CPB * j + n, n % 2
                if isinstance(c, int) and c < 0:
                    layernorm(j, n + 2)
                    return
                if not (isinstance(c, int) and c < 1):
                    add_linear(c - 1)
                dve.wait_ge(xnT_ready, c + 1)
                if isinstance(c, int) and c == 0:
                    dve.wait_ge(pads_stored, 32)
                if not (isinstance(c, int) and c < 1):
                    dve.wait_ge(y8_ready, c)
                nc.vector.tensor_scalar(quant[:], xnT[:, k], scales[:, 2:3], FP8_MAX, ALU.mult,
                                        ALU.min).then_inc(quant_chain, 1)
                dve.wait_ge(quant_chain, 3 * c + 1)
                nc.vector.tensor_scalar(quant[:], quant[:], -FP8_MAX, None, ALU.max).then_inc(quant_chain, 1)
                dve.wait_ge(quant_chain, 3 * c + 2)
                nc.vector.tensor_scalar(power[:].bitcast(I32), quant[:].bitcast(I32), 0x7F800000, None,
                                        ALU.bitwise_and).then_inc(quant_chain, 1)
                dve.wait_ge(quant_chain, 3 * c + 3)
                nc.vector.tensor_scalar(power[:], power[:], FP8_MIN_NORMAL, ROUND, ALU.max,
                                        ALU.mult).then_inc(power_ready, 1)
                cut(c, k, 0)
                layernorm(j, n + 2)
                cut(c, k, 1)
                for w in range(2):
                    dve.wait_ge(mid_ready, 2 * c + w + 1)
                    nc.vector.tensor_tensor(qk_parts[:, k, w, 2], rest[:, w], qk_parts[:, k, w, 1],
                                            ALU.subtract).then_inc(lo_ready, 1)

            layernorm(0, 0)
            chunks(dve, body)
            add_linear(B * CPB - 1)

        @block.tensor
        def _(pe):
            pe.wait_ge(c_loaded, 16 * 10)

            def body(j, n):
                c = CPB * j + n
                k, k1 = n % 2, (n + 1) % 2
                main = not (isinstance(c, int) and c < 0)
                ahead = not (isinstance(c, int) and c + 1 > B * CPB - 1)
                if main:
                    if isinstance(c, int) and c == 0:
                        pe.wait_ge(w_loaded, 48)
                    pe.wait_ge(xnT_ready, c + 1)
                    if not (isinstance(c, int) and c < 1):
                        pe.wait_ge(rest_ready, 2 * c - 1)
                    for m in range(KC):
                        for i in range(KC):
                            last = nc.tensor.matmul(ps_q[:, m], wq[:, i, m * P:(m + 1) * P], xnT[:, k, i],
                                                    start=(i == 0), stop=(i == KC - 1))
                    last.then_inc(q_ready, 1)
                if ahead:
                    pe.wait_ge(xn_ready, c + 2)
                    if not (isinstance(c, int) and c < 1):
                        pe.wait_ge(base_ready, c)
                    for i in range(KC):
                        for t in range(TT):
                            last = nc.tensor.transpose(ps_t[:, i, t * P:(t + 1) * P],
                                                       xn[:, k1, t, i * P:(i + 1) * P], keep["ident"][:])
                    last.then_inc(t_ready, 1)
                if main:
                    if not (isinstance(c, int) and c < 1):
                        pe.wait_ge(rest_ready, 2 * c)
                    grouped = xnT[:, k].rearrange("p i (g r) -> p i g r", r=STRIDE)
                    ns = CH // STRIDE
                    for m in range(KC):
                        for cols, keys in ((slice(0, ns), grouped[:, :, :, 0]), (slice(ns, CH), grouped[:, :, :, 1:])):
                            for i in range(KC):
                                last = nc.tensor.matmul(ps_k[:, m, cols], wk[:, i, m * P:(m + 1) * P], keys[:, i],
                                                        start=(i == 0), stop=(i == KC - 1))
                    last.then_inc(k_ready, 1)
                    if not (isinstance(c, int) and c < 1):
                        pe.wait_ge(v_copied, c)
                    for t in range(TT):
                        for i in range(KC):
                            last = nc.tensor.matmul(ps_v[:, t // 2, t % 2 * H:(t % 2 + 1) * H],
                                                    xnT[:, k, i, t * P:(t + 1) * P], wv[:, i],
                                                    start=(i == 0), stop=(i == KC - 1))
                    last.then_inc(v_ready, 1)
                    if isinstance(c, int) and c == 0:
                        pe.wait_ge(w8_ready, 1)
                    pe.wait_ge(y8_ready, c + 1)
                    if ahead:
                        pe.wait_ge(xnT_ready, c + 2)
                    else:
                        pe.wait_ge(base_ready, c)
                    for t in range(TT):
                        for i in range(KC):
                            for part in range(PARTS):
                                last = nc.tensor.matmul(ps_f[:, t // 2, t % 2 * H:(t % 2 + 1) * H],
                                                        y8[:, k, i, t * P:(t + 1) * P], w8_parts[:, part, i],
                                                        start=(i == 0 and part == 0),
                                                        stop=(i == KC - 1 and part == PARTS - 1))
                    last.then_inc(f_ready, 1)

            chunks(pe, body)


ROUNDS = NS // P + 1
SU = ROUNDS * HG
M_AT = 1
FIRST, LAST = -2, STEPS + 1


def v_units(s):
    units = []
    for r in range(ROUNDS):
        if r == M_AT and -1 <= s and s + 1 < STEPS:
            units.append(("negmax",))
        if s + 2 < STEPS:
            units += [("max", r * HG + h) for h in range(HG)]
    return units


def part_attend(nc, dram, keep):
    before = {FIRST: 0}
    for s in range(FIRST, LAST + 1):
        before[s + 1] = before[s] + len(v_units(s))

    class Step:

        def __init__(self, j, n):
            self.j, self.n = j, n

        def at(self, d=0):
            return 2 * CPB * self.j + self.n + d

        def exists(self, d=0):
            return not isinstance(self.at(d), int) or 0 <= self.at(d) < STEPS

        def queries(self, d=0):
            return (self.n + d) % CPB

        def iteration(self, d=0):
            return 2 * self.j + (self.n + d) // CPB

        def parity(self, d=0):
            return (self.n + d) // CPB % 2

        def half_iteration(self, d=0):
            return self.j + (self.n + d) // CPB // 2

        def half(self, d=0):
            return CPB * self.j + (self.n + d) // 2

        def units(self):
            return v_units(self.n)

        def unit(self, d, i):
            return 2 * CPB * len(v_units(2)) * self.j + before[self.n + d] + i + 1

        def unit_named(self, d, kind):
            return self.unit(d, v_units(self.n + d).index(kind))

        def bank_free(self, i):
            if i >= 3:
                return self.unit(0, i - 3)
            if self.n - 1 not in before or not v_units(self.n - 1):
                return None
            count = len(v_units(self.n - 1))
            return self.unit(-1, max(u for u in range(count) if u % 3 == i))

    def steps(eng, body):
        for n in range(FIRST, 2):
            body(Step(0, n))
        with eng.Fori(0, (STEPS - 8) // 8) as j:
            for n in range(2, 10):
                body(Step(j, n))
        for n in range(STEPS - 6, LAST + 1):
            body(Step(0, n))

    with ExitStack() as ctx:
        def sb(name, shape, dt=F32):
            return ctx.enter_context(nc.sbuf_tensor(name, shape, dt))

        def sem(name):
            return ctx.enter_context(nc.semaphore(name))

        ps = ctx.enter_context(nc.psum_tensor("ps_attend", [P, 8, CH], F32))
        ps_s = [ps[:, i] for i in range(3)]
        ps_v = [ps[:, 3 + i] for i in range(3)]
        ps_o = [ps[:, 6 + i] for i in range(2)]

        q_op = [keep["q_op"], sb("q_op1", [P, HG * S], BF16)]
        k_op = [keep["k_op"], sb("k_op1", [P, HG * S + 2 * WPAD], BF16)]
        v_op = [sb(f"v_op{i}", [P, NS // P + S // P, HG * VW]) for i in range(2)]
        probs = sb("probs", [P, ROUNDS, HG, CH])
        out_rows = sb("out_rows", [P, 2, CH])
        peak = sb("peak", [P, 2, HG, TT])
        top = sb("top", [P, HG, TT])
        top_rest = sb("top_rest", [P, HG, TT])
        negmax = sb("negmax", [P, 2, HG, PARTS, TT], BF16)
        negmax_rows = sb("negmax_rows", [P, 2, P], BF16)
        sums = sb("sums", [P, HG * CH // P])
        shares = sb("shares", [P, HG * CH // P])
        share_rows = sb("share_rows", [P, CH])
        scale = sb("scale", [P, 2])

        tails_set = sem("tails_set")
        ones_set = sem("ones_set")
        scale_ready = sem("scale_ready")
        qk_loaded = keep["qk_loaded"]
        v_loaded = [sem(f"v_loaded{i}") for i in range(2)]
        s_ready = sem("s_ready")
        exp_done = sem("exp_done")
        pv_done = sem("pv_done")
        out_copied = sem("out_copied")
        u_ready = sem("u_ready")
        u_used = sem("u_used")
        top_chain = sem("top_chain")
        negmax_ready = sem("negmax_ready")
        negmax_stored = sem("negmax_stored")
        negmax_loaded = sem("negmax_loaded")
        sums_stored = sem("sums_stored")
        sums_loaded = sem("sums_loaded")
        shares_ready = sem("shares_ready")
        shares_stored = sem("shares_stored")
        shares_loaded = sem("shares_loaded")
        attn_ready = sem("attn_ready")
        attn_stored = [sem(f"attn_stored{i}") for i in range(2)]

        block = ctx.enter_context(nc.Block())

        def window(tile):
            return NS - WPAD + WSTEP * tile

        @block.gpsimd
        def _(pool):
            for par in range(2):
                nc.gpsimd.memset(k_op[par][:, HG * S:], 0.0).then_inc(tails_set, 1)
                pool.wait_ge(tails_set, par + 1)
            for par in range(2):
                nc.gpsimd.memset(k_op[par][KR:KM, 0:HG * S], 1.0).then_inc(ones_set, 1)
                pool.wait_ge(ones_set, par + 1)

            def body(st):
                if st.n >= 2:
                    par = st.n % 2
                    pool.wait_ge(shares_loaded, 16 * st.at(-1))
                    nc.gpsimd.tensor_tensor(out_rows[:, par], out_rows[:, par], share_rows[:],
                                            ALU.mult).then_inc(attn_ready, 1)

            steps(pool, body)

        @block.sync
        def _(sp):
            def load_v(it, par, windows=range(-1, STRIDE - 1)):
                v = dram["v"][it]
                for r in windows:
                    if r < 0:
                        to, src = v_op[par][:, 0:NS // P, :], v[LOCAL:LOCAL + S, :].rearrange(
                            "(c p r) w -> r p c w", p=P, r=STRIDE)[0]
                    else:
                        to = v_op[par][r:WIN:STRIDE - 1, NS // P:, :]
                        src = bass.AP(tensor=v.tensor, offset=v.offset + (1 + r) * HG * VW,
                                      ap=[[STRIDE * HG * VW, WIN // 3], [P * HG * VW, S // P], [1, HG * VW]])
                    sp.dma_start(to, src).then_inc(v_loaded[par], 16)

            load_v(0, 0)

            def load_piece(st, piece):
                place, it, par = st.queries(), st.iteration(CPB), st.parity(CPB)
                if not (st.exists() and st.exists(CPB - place)):
                    return
                if place < 2:
                    if st.n >= CPB and place == piece == 0:
                        sp.wait_ge(s_ready, SU * st.at())
                    load_qk(sp, dram, {"q_op": q_op[par], "k_op": k_op[par], "qk_loaded": qk_loaded}, it, par,
                            ("k_op", "q_op")[place:place + 1], range(3 * piece, 3 * piece + 3))
                else:
                    if st.n >= CPB and place == 2 and piece == 0:
                        sp.wait_ge(pv_done, ROUNDS * st.at(-2))
                    r = 2 * (place - 2) + piece - 1
                    load_v(it, par, range(r, r + 1))

            def body(st):
                if st.n >= 2:
                    sp.wait_ge(shares_ready, st.at(-1))
                    sp.dma_start(dram["shares"].rearrange("h (p w) -> (h p) w", w=HG * CH // P), shares[:]
                                 ).then_inc(shares_stored, 16)
                    sp.wait_ge(shares_stored, 16 * st.at(-1))
                    sp.dma_start(share_rows[:], dram["shares"].unsqueeze(1).broadcast_to([HG, VW, CH])
                                 ).then_inc(shares_loaded, 16)
                load_piece(st, 0)
                if st.n >= 2:
                    sp.wait_ge(attn_ready, st.at(-1))
                    cols = slice(st.queries(-2) * CH, (st.queries(-2) + 1) * CH)
                    sp.dma_start(dram["attn"][st.iteration(-2), :, cols], out_rows[:, st.n % 2]
                                 ).then_inc(attn_stored[st.n % 2], 16)
                if st.n >= 1 and st.exists(-1):
                    sp.wait_ge(out_copied, st.at())
                    sp.dma_start(dram["sums"], out_rows[D::VW, (st.n - 1) % 2]).then_inc(sums_stored, 16)
                load_piece(st, 1)
                if st.n >= 1 and st.exists(-1):
                    sp.wait_ge(sums_stored, 16 * st.at())
                    sp.dma_start(sums[:], dram["sums"].rearrange("h (p w) -> (h p) w", w=HG * CH // P)
                                 ).then_inc(sums_loaded, 16)

            steps(sp, body)
            for k in range(2):
                sp.wait_ge(attn_stored[k], 16 * STEPS // 2)

        @block.scalar
        def _(act):
            nc.scalar.activation(scale[:, 0:1], keep["unity"][:], ACT.Tanh, scale=0.5).then_inc(scale_ready, 1)
            act.wait_ge(scale_ready, 2)

            def copy_out(st):
                act.wait_ge(pv_done, ROUNDS * st.at())
                if st.n >= 3:
                    act.wait_ge(attn_stored[(st.n - 1) % 2], 16 * st.half(-1))
                nc.scalar.activation(out_rows[:, (st.n - 1) % 2], ps_o[(st.n - 1) % 2], ACT.Copy).then_inc(out_copied, 1)

            def body(st):
                for r in range(ROUNDS):
                    for h in range(HG):
                        if st.exists():
                            i = r * HG + h
                            act.wait_ge(s_ready, SU * st.at() + i + 1)
                            if h == 0 and st.n >= 1:
                                act.wait_ge(pv_done, ROUNDS * st.at(-1) + r + 1)
                            rows = P if r < ROUNDS - 1 else WIN
                            nc.scalar.activation(probs[0:rows, r, h], ps_s[i % 3][0:rows], ACT.Exp,
                                                 scale=scale[0:rows, 1:2]).then_inc(exp_done, 1)
                        if r == 2 and h == 1 and st.exists(-1):
                            copy_out(st)
                        if ("negmax",) in st.units() and r == 2 and h == 0:
                            par = st.n % 2
                            act.wait_ge(u_used, st.unit_named(0, ("negmax",)))
                            if st.n >= 1:
                                act.wait_ge(negmax_loaded, 16 * st.at(0))
                            act.dma_start(dram["negmax"][par].rearrange("k (t q) -> (k t) q", q=P),
                                          negmax_rows[0:HG * PARTS * TT, par]).then_inc(negmax_stored, 16)
                        if ("negmax",) in st.units() and r == 3 and h == 2:
                            cols = slice(st.queries(1) * CH, (st.queries(1) + 1) * CH)
                            act.wait_ge(negmax_stored, 16 * st.at(2))
                            act.dma_start(
                                q_op[st.parity(1)][KR:KM, :].rearrange("p (h s) -> p h s", h=HG)[:, :, cols],
                                dram["negmax"][st.n % 2].rearrange("(h a) s -> a h s", a=PARTS)
                                ).then_inc(negmax_loaded, 16)

            steps(act, body)

        @block.vector
        def _(dve):
            dve.wait_ge(scale_ready, 1)
            nc.vector.tensor_scalar(scale[:, 1:2], scale[:, 0:1], 0.5 * D ** -0.5, 0.5 * D ** -0.5, ALU.mult,
                                    ALU.add).then_inc(scale_ready, 1)

            def body(st):
                units = st.units()

                def turn_sums():
                    dve.wait_ge(sums_loaded, 16 * st.at(-1))
                    if st.n >= 3:
                        dve.wait_ge(shares_stored, 16 * st.at(-2))
                    nc.vector.reciprocal(shares[:], sums[:]).then_inc(shares_ready, 1)

                if st.n >= 2 and not units:
                    turn_sums()
                for i, unit in enumerate(units):
                    if st.n >= 2 and i == min(HG, len(units)) - 1:
                        turn_sums()
                    src = ps_v[i % 3]
                    dve.wait_ge(u_ready, st.unit(0, i))
                    if unit[0] == "max":
                        m = unit[1]
                        h = m % HG
                        if m < TT * HG:
                            ins = nc.vector.tensor_reduce(peak[:, 0, h, m // HG:m // HG + 1], src, AX_X, ALU.max)
                        else:
                            ins = nc.vector.tensor_reduce(
                                peak[:, 1, h], src[:, 0:TT * WIN].rearrange("p (t w) -> p t w", t=TT), AX_X, ALU.max)
                    else:
                        par = st.n % 2
                        if st.n >= 1:
                            dve.wait_ge(negmax_stored, 16 * st.at())
                        ins = nc.vector.tensor_copy(negmax_rows[0:HG * PARTS * TT, par],
                                                    src[0:HG * PARTS * TT, 0:P])
                    ins.then_inc(u_used, 1)
                if st.exists(2):
                    dve.wait_ge(u_used, st.unit(0, len(units) - 1))
                    done = 4 * st.at(2)
                    parts = negmax[:, st.n % 2]
                    nc.vector.tensor_tensor(top[:], peak[:, 0], peak[:, 1], ALU.max).then_inc(top_chain, 1)
                    dve.wait_ge(top_chain, done + 1)
                    nc.vector.tensor_scalar(parts[:, :, 0], top[:], -1.0, None, ALU.mult).then_inc(top_chain, 1)
                    dve.wait_ge(top_chain, done + 2)
                    nc.vector.scalar_tensor_tensor(top_rest[:], top[:], -1.0, parts[:, :, 0], ALU.mult,
                                                   ALU.subtract).then_inc(top_chain, 1)
                    dve.wait_ge(top_chain, done + 3)
                    nc.vector.tensor_copy(parts[:, :, 1], top_rest[:]).then_inc(top_chain, 1)
                    dve.wait_ge(top_chain, done + 4)
                    nc.vector.tensor_tensor(parts[:, :, 2], top_rest[:], parts[:, :, 1],
                                            ALU.subtract).then_inc(negmax_ready, 1)

            steps(dve, body)

        @block.tensor
        def _(pe):
            def score(st, r, h):
                i = r * HG + h
                q, k, q0 = q_op[st.parity()], k_op[st.parity()], h * S + st.queries() * CH
                if i == 0:
                    pe.wait_ge(negmax_loaded, 16 * st.at(1))
                    if st.n == 0:
                        pe.wait_ge(ones_set, 2)
                if i >= 3:
                    pe.wait_ge(exp_done, SU * st.at() + i - 2)
                elif st.n >= 1:
                    pe.wait_ge(exp_done, SU * st.at(-1) + {0: 19, 1: 20, 2: 18}[i])
                if r < ROUNDS - 1:
                    ins = nc.tensor.matmul(ps_s[i % 3], k[0:KM, h * S + r * P:h * S + (r + 1) * P],
                                           q[0:KM, q0:q0 + CH], start=True, stop=True)
                else:
                    mask = {0: 0, CPB - 1: 2}.get(st.queries(), 1)
                    nc.tensor.matmul(ps_s[i % 3][0:WIN], keep["ident_bf"][0:WIN, 0:WIN], keep["key_mask"][0:WIN, mask],
                                     start=True, stop=False)
                    for t in range(TT):
                        at = h * S + window(st.queries() * TT + t)
                        ins = nc.tensor.matmul(ps_s[i % 3][0:WIN, t * P:(t + 1) * P], k[0:KM, at:at + WIN],
                                               q[0:KM, q0 + t * P:q0 + (t + 1) * P], start=False, stop=(t == TT - 1))
                ins.then_inc(s_ready, 1)

            def unit(st, i, kind, m):
                bank = ps_v[i % 3]
                free = st.bank_free(i)
                if free is not None:
                    pe.wait_ge(u_used, free)
                if kind == "max":
                    q, k = q_op[st.parity(2)], k_op[st.parity(2)]
                    t, h = m // HG, m % HG
                    q0 = h * S + st.queries(2) * CH
                    if m == 0 and st.queries(2) == 0:
                        pe.wait_ge(qk_loaded[st.parity(2)], 16 * QK_LOADS * (st.half_iteration(2) + 1))
                    if t < TT:
                        ins = nc.tensor.matmul(bank, q[0:KR, q0 + t * P:q0 + (t + 1) * P],
                                               k[0:KR, h * S:h * S + NS], start=True, stop=True)
                    else:
                        mask = {0: 0, CPB - 1: 2}.get(st.queries(2), 1)
                        nc.tensor.matmul(bank[:, 0:TT * WIN], keep["ident_bf"][:], keep["max_mask"][:, mask],
                                         start=True, stop=False)
                        for t in range(TT):
                            at = h * S + window(st.queries(2) * TT + t)
                            ins = nc.tensor.matmul(bank[:, t * WIN:(t + 1) * WIN], q[0:KR, q0 + t * P:q0 + (t + 1) * P],
                                                   k[0:KR, at:at + WIN], start=False, stop=(t == TT - 1))
                else:
                    pe.wait_ge(negmax_ready, st.at(2))
                    parts = negmax[:, (st.n + 1) % 2].rearrange("p h a t -> p (h a t)")
                    ins = nc.tensor.matmul(bank[0:HG * PARTS * TT, 0:P], parts, keep["ident_bf"][:],
                                           start=True, stop=True)
                ins.then_inc(u_ready, 1)

            def weigh(st, d, r):
                out, v = ps_o[(st.n + d) % 2], v_op[st.parity(d)]
                if r == 0:
                    if st.queries(d) == 0:
                        pe.wait_ge(v_loaded[st.parity(d)], 64 * (st.half_iteration(d) + 1))
                    if st.n + d >= 2:
                        pe.wait_ge(out_copied, st.at(d - 1))
                if r < ROUNDS - 1:
                    pe.wait_ge(exp_done, SU * st.at(d) + (r + 1) * HG)
                    for h in range(HG):
                        ins = nc.tensor.matmul(out[h * VW:(h + 1) * VW], v[:, r, h * VW:(h + 1) * VW], probs[:, r, h],
                                               start=(r == 0), stop=False)
                else:
                    pe.wait_ge(exp_done, SU * st.at(d + 1))
                    for t in range(TT):
                        tile = NS // P + st.queries(d) * TT + t
                        for h in range(HG):
                            ins = nc.tensor.matmul(out[h * VW:(h + 1) * VW, t * P:(t + 1) * P],
                                                   v[0:WIN, tile, h * VW:(h + 1) * VW],
                                                   probs[0:WIN, r, h, t * P:(t + 1) * P],
                                                   start=False, stop=(t == TT - 1))
                ins.then_inc(pv_done, 1)

            def body(st):
                units = list(enumerate(st.units()))

                def next_unit():
                    i, u = units.pop(0)
                    unit(st, i, u[0], u[-1])

                for r in range(ROUNDS):
                    if r == M_AT and units and units[0][1] == ("negmax",):
                        next_unit()
                    for h in range(HG):
                        if st.exists():
                            score(st, r, h)
                        if units and units[0][1][0] == "max":
                            next_unit()
                    if r >= 2 and st.exists():
                        weigh(st, 0, r - 2)
                    if r < 2 and st.exists(-1):
                        weigh(st, -1, r + 3)

            pe.wait_ge(tails_set, 2)
            steps(pe, body)


def part_finish(nc, io, dram, keep, out):
    with ExitStack() as ctx:
        def sb(name, shape, dt=F32):
            return ctx.enter_context(nc.sbuf_tensor(name, shape, dt))

        def sem(name):
            return ctx.enter_context(nc.semaphore(name))

        ps = ctx.enter_context(nc.psum_tensor("ps_finish", [P, 8, CH], F32))
        ps_y = [ps[:, 2 * i:2 * i + 2] for i in range(4)]
        heads = sb("heads", [P, CPB, KC, CH])
        heads_loaded = [sem(f"heads_loaded{i}") for i in range(CPB)]
        y_ready = sem("y_ready")
        total_ready = sem("total_ready")
        out_stored = sem("out_stored")
        base = keep["base"].rearrange("p (c t) f -> p c (t f)", t=TT)
        out_rows = out.rearrange("b (c t p) f -> (b c) p t f", t=TT, p=P)
        block = ctx.enter_context(nc.Block())

        @block.sync
        def _(sp):
            def load(j, n):
                for i in range(KC):
                    rows = dram["attn"][bass.ds(j * G + 2 * i, 2), :, n * CH:(n + 1) * CH].rearrange(
                        "g (h r) s -> (g h) r s", r=VW)
                    sp.dma_start(heads[:, n, i], rows[:, 0:D]).then_inc(heads_loaded[n], 16)

            for n in range(CPB):
                load(0, n)
            with sp.Fori(1, B) as j:
                for n in range(CPB):
                    sp.wait_ge(y_ready, CPB * j + n - CPB + 1)
                    load(j, n)

        @block.tensor
        def _(pe):
            def body(j, n):
                c = CPB * j + n
                pe.wait_ge(heads_loaded[n], 16 * KC * (j + 1))
                if not isinstance(j, int):
                    pe.wait_ge(total_ready, c - CPB + 1)
                for t in range(TT):
                    for i in range(KC):
                        last = nc.tensor.matmul(ps_y[n][:, t // 2, t % 2 * H:(t % 2 + 1) * H],
                                                heads[:, n, i, t * P:(t + 1) * P], keep["wo"][:, i],
                                                start=(i == 0), stop=(i == KC - 1))
                last.then_inc(y_ready, 1)

            for n in range(CPB):
                body(0, n)
            with pe.Fori(1, B) as j:
                for n in range(CPB):
                    body(j, n)

        @block.vector
        def _(dve):
            with dve.Fori(0, B) as j:
                for n in range(CPB):
                    c = CPB * j + n
                    dve.wait_ge(y_ready, c + 1)
                    nc.vector.tensor_tensor(base[:, c], ps_y[n].rearrange("p a f -> p (a f)"), base[:, c],
                                            ALU.add).then_inc(total_ready, 1)

        @block.scalar
        def _(act):
            with act.Fori(0, B) as j:
                for n in range(CPB):
                    c = CPB * j + n
                    act.wait_ge(total_ready, c + 1)
                    act.dma_start(out_rows[c], keep["base"].rearrange("p (c t) f -> p c t f", t=TT)[:, c]
                                  ).then_inc(out_stored, 16)
            act.wait_ge(out_stored, 16 * B * CPB)


def build(nc, io, out):
    dram = {
        "qk": [nc.dram_tensor(f"{n}_parts_dram", [PARTS, NIT, HG * D, S], BF16).ap() for n in "qk"],
        "v": nc.dram_tensor("v_dram", [NIT, LOCAL + S + LOCAL, HG * VW], F32).ap(),
        "attn": nc.dram_tensor("attn_dram", [NIT, HG * VW, S], F32).ap(),
        "sums": nc.dram_tensor("sums_dram", [HG, CH], F32).ap(),
        "shares": nc.dram_tensor("shares_dram", [HG, CH], F32).ap(),
        "negmax": nc.dram_tensor("negmax_dram", [2, HG * PARTS, CH], BF16).ap(),
    }
    with ExitStack() as ctx:
        def sb(name, shape, dt=F32):
            return ctx.enter_context(nc.sbuf_tensor(name, shape, dt))

        keep = {
            "ident": sb("ident", [P, P]),
            "ident_bf": sb("ident_bf", [P, P], BF16),
            "max_mask": sb("max_mask", [P, MASKS, TT * WIN], BF16),
            "key_mask": sb("key_mask", [P, MASKS, CH], BF16),
            "base": sb("base", [P, B * S // P, H]),
            "q_op": sb("q_op0", [P, HG * S], BF16),
            "k_op": sb("k_op0", [P, HG * S + 2 * WPAD], BF16),
            "qk_loaded": [ctx.enter_context(nc.semaphore(f"qk_loaded{i}")) for i in range(2)],
            "wo": sb("wo", [P, KC, H]),
            "unity": sb("unity", [P, 1]),
        }
        part_project(nc, io, dram, keep)
        part_attend(nc, dram, keep)
        part_finish(nc, io, dram, keep, out)


def kernel(L0_attn_x, L0_attn_q_w, L0_attn_k_w, L0_attn_v_w, L0_attn_o_w, L0_attn_o_b, L0_attn_unity_scale,
           L0_ffn_weight_fp8, L0_ffn_bias, L0_ffn_input_scale, L0_ffn_weight_scale):
    import numpy as np
    import concourse.bacc as bacc
    from concourse.bass_utils import run_bass_kernel_spmd

    q = np.arange(P)
    key = np.arange(WIN)
    rel = STRIDE * (key // 3) + 1 + key % 3 - LOCAL
    near = np.abs(rel[:, None] - q[None, :]) <= LOCAL
    seen = np.stack([np.stack([near] * TT, 1)] * MASKS)
    seen[0, :, 0] &= (rel >= 0)[:, None]
    seen[MASKS - 1, :, TT - 1] &= (rel < P)[:, None]
    key_mask = np.where(seen, np.float32(0), np.float32(-BIG)).reshape(MASKS, WIN, CH)
    max_mask = np.where(seen.transpose(0, 3, 2, 1), np.float32(0), np.float32(-BIG)).reshape(MASKS, P, TT * WIN)

    def columns(w):
        w = np.asarray(w).reshape(H, KC, G // KC, HG, D)
        return np.ascontiguousarray(w.transpose(0, 1, 2, 4, 3)).reshape(H, H)

    arrays = {
        "x": np.asarray(L0_attn_x),
        "q_w": columns(L0_attn_q_w),
        "k_w": columns(L0_attn_k_w),
        "v_w": np.asarray(L0_attn_v_w),
        "o_w": np.asarray(L0_attn_o_w),
        "o_b": np.asarray(L0_attn_o_b),
        "unity": np.asarray(L0_attn_unity_scale).reshape(1),
        "w8T": np.ascontiguousarray(np.asarray(L0_ffn_weight_fp8).T),
        "ffn_bias": np.asarray(L0_ffn_bias),
        "input_scale": np.asarray(L0_ffn_input_scale),
        "weight_scale": np.asarray(L0_ffn_weight_scale),
        "ident": np.eye(P, dtype=np.float32),
        "max_mask": np.ascontiguousarray(max_mask),
        "key_mask": np.ascontiguousarray(key_mask),
    }
    nc = bacc.Bacc("TRN2", target_bir_lowering=False, num_devices=1)
    io = {n: nc.dram_tensor(f"in_{n}", a.shape, mybir.dt.from_np(a.dtype), kind="ExternalInput").ap()
          for n, a in arrays.items()}
    out = nc.dram_tensor("out", [B, S, H], F32, kind="ExternalOutput").ap()
    build(nc, io, out)
    r = run_bass_kernel_spmd(nc, [{f"in_{n}": a for n, a in arrays.items()}], core_ids=[0])
    return r.results[0]["out"]
```

```python
from contextlib import ExitStack

import concourse.bass as bass
from concourse import mybir

F32 = mybir.dt.float32
BF16 = mybir.dt.bfloat16
F16 = mybir.dt.float16
I32 = mybir.dt.int32
ALU = mybir.AluOpType
ACT = mybir.ActivationFunctionType
AX_X = mybir.AxisListType.X

B, S, H = 4, 2048, 256
NH, D = 16, 16
P = 128
KC = H // P
CH = 512
TT = CH // P
CPB = S // CH
G, HG = 4, 4
NIT = B * G
STEPS = NIT * CPB
STRIDE, LOCAL = 4, 8
NS = S // STRIDE
WIN = (P + 2 * LOCAL) // STRIDE * (STRIDE - 1)
WSTEP = P // STRIDE * (STRIDE - 1)
WPAD = LOCAL // STRIDE * (STRIDE - 1)
PARTS = 3
KR = 6 * D
KM = KR + PARTS
QK_LOADS = 2 * 6
VW = 2 * D
EPS = 1e-5
FP8_MAX = 448.0
FP8_MIN_NORMAL = 2.0 ** -6
ROUND = 1.5 * 2.0 ** 20
BIG = 1e30
MASKS = 3


def chunks(eng, body):
    for n in range(-1, 3):
        body(0, n)
    with eng.Fori(0, B - 2) as j:
        for n in range(3, 3 + CPB):
            body(j, n)
    for n in range(B * CPB - CPB - 1, B * CPB):
        body(0, n)


def load_qk(eng, dram, operands, it, par, which=("k_op", "q_op"), rows=range(6)):
    q, k = dram["qk"]

    for op, source, parts in (("k_op", k, (0, 1, 2, 0, 1, 0)), ("q_op", q, (0, 0, 0, 1, 1, 2))):
        for i in rows if op in which else ():
            part = parts[i]
            eng.dma_start(operands[op][i * D:(i + 1) * D, 0:HG * S],
                          source[part, it].rearrange("(r h) s -> r (h s)", h=HG)
                          ).then_inc(operands["qk_loaded"][par], 16)


def part_project(nc, io, dram, keep):
    with ExitStack() as ctx:
        def sb(name, shape, dt=F32):
            return ctx.enter_context(nc.sbuf_tensor(name, shape, dt))

        def sem(name):
            return ctx.enter_context(nc.semaphore(name))

        ps = ctx.enter_context(nc.psum_tensor("ps_project", [P, 8, CH], F32))
        ps_q, ps_t, ps_k, ps_v = (ps[:, 2 * i:2 * i + 2, :] for i in range(4))
        ps_f = ps_t

        wq, wk, wv = (sb(n, [P, KC, H]) for n in ("wq", "wk", "wv"))
        w8 = sb("w8", [P, KC, H])
        w8_parts = sb("w8_parts", [P, 2, KC, H], F16)
        bias = sb("bias", [P, H])
        bias_o = sb("bias_o", [P, H])
        scales = sb("scales", [P, 4])
        x_in = sb("x_in", [P, 2, TT, H])
        stats = sb("stats", [P, TT, 6])
        counts = sb("counts", [P, TT])
        mv = sb("mv", [P, TT, 2])
        var = sb("var", [P, TT])
        dev = sb("dev", [P, TT])
        newton = sb("newton", [P, 3, TT])
        rstd = sb("rstd", [P, TT])
        xn = sb("xn", [P, 2, TT, H])
        xnT = sb("xnT", [P, 2, KC, CH])
        qk_parts = sb("qk_parts", [P, 2, 2, PARTS, KC, CH], BF16)
        rest = sb("rest", [P, 2, KC, CH])
        v_sb = sb("v_sb", [P, 2, TT, NH, VW])
        quant = sb("quant", [P, KC, CH])
        power = sb("power", [P, KC, CH])
        y8 = sb("y8", [P, 2, KC, CH], F16)

        w_loaded = sem("w_loaded")
        scales_loaded = sem("scales_loaded")
        ident_loaded = sem("ident_loaded")
        w8_loaded = sem("w8_loaded")
        rest_loaded = sem("rest_loaded")
        masks_ready = sem("masks_ready")
        ones_set = sem("first_ones_set")
        zeros_set = sem("zeros_set")
        v_set = sem("v_set")
        pads_stored = sem("pads_stored")
        setup = sem("setup")
        w8_ready = sem("w8_ready")
        bias_ready = sem("bias_ready")
        x_loaded = [sem(f"x_loaded{i}") for i in range(2)]
        stat = sem("stat")
        var_ready = sem("var_ready")
        dev_ready = sem("dev_ready")
        xn_ready = sem("xn_ready")
        t_ready = sem("t_ready")
        xnT_ready = sem("xnT_ready")
        q_ready = sem("q_ready")
        k_ready = sem("k_ready")
        v_ready = sem("v_ready")
        f_ready = sem("f_ready")
        hi_ready = sem("hi_ready")
        rest_ready = sem("rest_ready")
        mid_ready = sem("mid_ready")
        lo_ready = sem("lo_ready")
        v_copied = sem("v_copied")
        quant_chain = sem("quant_chain")
        power_ready = sem("power_ready")
        sum_ready = sem("sum_ready")
        y8_ready = sem("y8_ready")
        xb_ready = sem("xb_ready")
        base_ready = sem("base_ready")
        qk_stored = [sem(f"qk_stored{i}") for i in range(2)]
        v_stored = [sem(f"v_stored{i}") for i in range(2)]

        x_rows = io["x"].rearrange("b (c t p) f -> (b c) p t f", t=TT, p=P)
        base = keep["base"].rearrange("p (c t) f -> p c (t f)", t=TT)
        spare = keep["base"].rearrange("p t f -> p (t f)")[:, (B - 1) * S // P * H:]
        key_mask_f = spare[:, 0:MASKS * CH].rearrange("p (m n) -> p m n", m=MASKS)
        max_mask_f = spare[:, MASKS * CH:MASKS * (CH + TT * WIN)].rearrange("p (m n) -> p m n", m=MASKS)
        zeros = spare[0:NIT, -LOCAL * HG * VW // 2:]
        block = ctx.enter_context(nc.Block())

        def half(j, n):
            return CPB // 2 * j + n // 2

        @block.sync
        def _(sp):
            sp.dma_start(x_in[:, 0], x_rows[0]).then_inc(x_loaded[0], 16)
            sp.dma_start(scales[:, 0:1], io["input_scale"].partition_broadcast(P)).then_inc(scales_loaded, 16)
            sp.dma_start(scales[:, 1:2], io["weight_scale"].partition_broadcast(P)).then_inc(scales_loaded, 16)
            sp.dma_start(bias[:], io["ffn_bias"].partition_broadcast(P)).then_inc(scales_loaded, 16)
            sp.dma_start(bias_o[:], io["o_b"].partition_broadcast(P)).then_inc(scales_loaded, 16)
            sp.dma_start(keep["ident"][:], io["ident"]).then_inc(ident_loaded, 16)
            sp.dma_start(x_in[:, 1], x_rows[1]).then_inc(x_loaded[1], 16)
            for w, name in ((wq, "q_w"), (wk, "k_w"), (wv, "v_w")):
                sp.dma_start(w[:], io[name].rearrange("(k p) f -> p k f", p=P)).then_inc(w_loaded, 16)
            sp.dma_start(w8[:], io["w8T"].rearrange("(k p) f -> p k f", p=P)).then_inc(w8_loaded, 16)
            sp.dma_start(keep["unity"][:], io["unity"].partition_broadcast(P)).then_inc(rest_loaded, 16)
            sp.dma_start(max_mask_f, io["max_mask"].rearrange("m p n -> p m n")).then_inc(rest_loaded, 16)
            sp.dma_start(key_mask_f[0:WIN], io["key_mask"].rearrange("m p n -> p m n")).then_inc(rest_loaded, 16)
            sp.dma_start(keep["wo"][:], io["o_w"].rearrange("(k p) f -> p k f", p=P)).then_inc(rest_loaded, 16)
            sp.wait_ge(zeros_set, 1)
            for edge in (0, LOCAL + S):
                for half_edge in range(2):
                    rows = slice(edge + half_edge * LOCAL // 2, edge + (half_edge + 1) * LOCAL // 2)
                    sp.dma_start(dram["v"][:, rows, :].rearrange("i t w -> i (t w)"), zeros).then_inc(pads_stored, 16)

            def body(j, n):
                c = CPB * j + n
                if not (isinstance(c, int) and c + 3 > B * CPB - 1):
                    sp.wait_ge(xn_ready, c + 2)
                    sp.wait_ge(xb_ready, c + 2)
                    sp.dma_start(x_in[:, (n + 1) % 2], x_rows[c + 3]).then_inc(x_loaded[(n + 1) % 2], 16)
                if isinstance(c, int) and c < 0:
                    return
                b4, cq, k = (j + n // CPB) * G, n % CPB, n % 2
                pair = (j + n // CPB) * KC
                ns = CH // STRIDE
                for w, part in ((0, 0), (0, 1), (1, 0), (0, 2), (1, 1), (None, None), (1, 2)):
                    if w is None:
                        sp.wait_ge(v_copied, c + 1)
                        for t in range(TT):
                            row = LOCAL + cq * CH + t * P
                            sp.dma_start(dram["v"][bass.ds(b4, G), row:row + P, :].rearrange("g p w -> p g w"),
                                         v_sb[:, k, t].rearrange("p (g h) w -> p g (h w)", g=G)).then_inc(v_stored[k], 16)
                        continue
                    sp.wait_ge((hi_ready, mid_ready, lo_ready)[part], 2 * c + w + 1)
                    spans = [(cq * ns, 0, ns), (NS + cq * (CH - ns), ns, CH)] if w else [(cq * CH, 0, CH)]
                    pairs = dram["qk"][w][part].rearrange("(m u) r s -> m (u r) s", u=2)
                    for to, a, e in spans:
                        sp.dma_start(
                            pairs[bass.ds(pair, KC), :, to:to + e - a].rearrange("m r s -> r m s"),
                            qk_parts[:, k, w, part, :, a:e]).then_inc(qk_stored[k], 16)
                if isinstance(c, int) and c == B * CPB - CPB:
                    for par in range(2):
                        sp.wait_ge(qk_stored[par], 16 * 9 * half(j, n))
                    load_qk(sp, dram, keep, 0, 0)

            chunks(sp, body)
            sp.wait_ge(pads_stored, 16 * 4)
            for k in range(2):
                sp.wait_ge(qk_stored[k], 16 * 9 * B * CPB // 2)
                sp.wait_ge(v_stored[k], 16 * TT * B * CPB // 2)

        @block.gpsimd
        def _(pool):
            nc.gpsimd.memset(zeros, 0.0).then_inc(zeros_set, 1)
            nc.gpsimd.memset(v_sb[:, 0, :, :, D:VW], 1.0).then_inc(v_set, 1)
            nc.gpsimd.memset(v_sb[:, 1, :, :, D:VW], 1.0).then_inc(v_set, 1)
            pool.wait_ge(bias_ready, 3)

            def body(j, n):
                c = CPB * j + n
                k, k1 = n % 2, (n + 1) % 2
                if not (isinstance(c, int) and c + 1 > B * CPB - 1):
                    pool.wait_ge(x_loaded[k1], 16 * (half(j, n + 1) + 1))
                    nc.gpsimd.tensor_tensor(base[:, c + 1].rearrange("p (t f) -> p t f", t=TT), x_in[:, k1],
                                            bias[:].unsqueeze(1).broadcast_to([P, TT, H]),
                                            ALU.add).then_inc(xb_ready, 1)
                if isinstance(c, int) and c < 0:
                    return
                pool.wait_ge(power_ready, c + 1)
                nc.gpsimd.tensor_tensor(quant[:], quant[:], power[:], ALU.add).then_inc(sum_ready, 1)
                pool.wait_ge(sum_ready, c + 1)
                if not (isinstance(c, int) and c < 2):
                    pool.wait_ge(f_ready, c - 1)
                nc.gpsimd.tensor_tensor(y8[:, k], quant[:], power[:], ALU.subtract).then_inc(y8_ready, 1)
                if isinstance(c, int) and c == 1:
                    pool.wait_ge(y8_ready, 2)
                    nc.gpsimd.memset(keep["k_op"][KR:KM, 0:HG * S], 1.0).then_inc(ones_set, 1)
                    pool.wait_ge(ones_set, 1)
                if isinstance(c, int) and c == 0:
                    pool.wait_ge(rest_loaded, 16 * 4)
                    nc.gpsimd.tensor_copy(keep["max_mask"][:], max_mask_f).then_inc(masks_ready, 1)
                    nc.gpsimd.tensor_copy(keep["key_mask"][0:WIN], key_mask_f[0:WIN]).then_inc(masks_ready, 1)
                    nc.gpsimd.tensor_copy(keep["ident_bf"][:], keep["ident"][:]).then_inc(masks_ready, 1)
                    pool.wait_ge(masks_ready, 3)
                    pool.wait_ge(pads_stored, 16 * 4)

            chunks(pool, body)

        @block.scalar
        def _(act):
            def deviation(j, n, d):
                c = CPB * j + n + d
                if not (isinstance(c, int) and c > B * CPB - 1):
                    act.wait_ge(var_ready, c + 1)
                    nc.scalar.activation(dev[:], var[:], ACT.Sqrt).then_inc(dev_ready, 1)

            def body(j, n):
                c = CPB * j + n
                k = n % 2
                main = not (isinstance(c, int) and c < 0)
                ahead = not (isinstance(c, int) and c + 1 > B * CPB - 1)
                if main:
                    act.wait_ge(q_ready, c + 1)
                    if not (isinstance(c, int) and c < 2):
                        act.wait_ge(qk_stored[k], 16 * 9 * half(j, n))
                    nc.scalar.activation(qk_parts[:, k, 0, 0], ps_q, ACT.Copy).then_inc(hi_ready, 1)
                if ahead:
                    act.wait_ge(t_ready, c + 2)
                    if not (isinstance(c, int) and c < 1):
                        act.wait_ge(v_ready, c)
                        act.wait_ge(power_ready, c)
                    nc.scalar.activation(xnT[:, (n + 1) % 2], ps_t, ACT.Copy).then_inc(xnT_ready, 1)
                if main:
                    act.wait_ge(rest_ready, 2 * c + 1)
                    nc.scalar.activation(qk_parts[:, k, 0, 1], rest[:, 0], ACT.Copy).then_inc(mid_ready, 1)
                deviation(j, n, 2)
                if main:
                    act.wait_ge(k_ready, c + 1)
                    nc.scalar.activation(qk_parts[:, k, 1, 0], ps_k, ACT.Copy).then_inc(hi_ready, 1)
                    act.wait_ge(rest_ready, 2 * c + 2)
                    nc.scalar.activation(qk_parts[:, k, 1, 1], rest[:, 1], ACT.Copy).then_inc(mid_ready, 1)
                    act.wait_ge(v_ready, c + 1)
                    if isinstance(c, int) and c == 0:
                        act.wait_ge(v_set, 2)
                    if not (isinstance(c, int) and c < 2):
                        act.wait_ge(v_stored[k], 16 * TT * half(j, n))
                    nc.scalar.activation(
                        v_sb[:, k].rearrange("p t h w -> p (t h) w")[:, :, 0:D],
                        ps_v.rearrange("p a (t w) -> p (a t) w", w=D), ACT.Copy).then_inc(v_copied, 1)

            deviation(0, -1, 1)
            chunks(act, body)

        @block.vector
        def _(dve):
            def prepare_linear():
                dve.wait_ge(w8_loaded, 16)
                nc.vector.tensor_copy(w8_parts[:, 0], w8[:]).then_inc(setup, 1)
                dve.wait_ge(setup, 1)
                nc.vector.tensor_tensor(w8_parts[:, 1], w8[:], w8_parts[:, 0], ALU.subtract).then_inc(w8_ready, 1)

            def add_linear(c):
                dve.wait_ge(f_ready, c + 1)
                dve.wait_ge(xb_ready, c + 1)
                nc.vector.scalar_tensor_tensor(base[:, c], ps_f.rearrange("p a f -> p (a f)"), scales[:, 3:4],
                                               base[:, c], ALU.mult, ALU.add).then_inc(base_ready, 1)

            def layernorm(j, n):
                c, k = CPB * j + n, n % 2
                if isinstance(c, int) and c > B * CPB - 1:
                    return
                done = 7 * c
                dve.wait_ge(x_loaded[k], 16 * (half(j, n) + 1))
                for t in range(TT):
                    last = nc.vector.bn_stats(stats[:, t], x_in[:, k, t])
                last.then_inc(stat, 1)
                dve.wait_ge(stat, done + 1)
                nc.vector.tensor_copy(counts[:], stats[:, :, 0])
                for t in range(TT):
                    last = nc.vector.bn_aggr(mv[:, t], stats[:, t])
                last.then_inc(stat, 1)
                dve.wait_ge(stat, done + 2)
                nc.vector.tensor_scalar(var[:], mv[:, :, 1], EPS, None, ALU.add).then_inc(var_ready, 1)
                dve.wait_ge(dev_ready, c + 1)
                nc.vector.reciprocal(newton[:, 0], dev[:]).then_inc(stat, 1)
                dve.wait_ge(stat, done + 3)
                nc.vector.tensor_tensor(newton[:, 1], newton[:, 0], newton[:, 0], ALU.mult).then_inc(stat, 1)
                dve.wait_ge(stat, done + 4)
                nc.vector.tensor_tensor(newton[:, 2], newton[:, 1], var[:], ALU.mult).then_inc(stat, 1)
                dve.wait_ge(stat, done + 5)
                nc.vector.tensor_scalar(newton[:, 1], newton[:, 2], -0.5, 1.5, ALU.mult, ALU.add).then_inc(stat, 1)
                dve.wait_ge(stat, done + 6)
                nc.vector.tensor_tensor(rstd[:], newton[:, 1], newton[:, 0], ALU.mult).then_inc(stat, 1)
                dve.wait_ge(stat, done + 7)
                if not (isinstance(c, int) and c < 2):
                    dve.wait_ge(t_ready, c - 1)
                for t in range(TT):
                    last = nc.vector.tensor_scalar(xn[:, k, t], x_in[:, k, t], mv[:, t, 0:1],
                                                   rstd[:, t:t + 1], ALU.subtract, ALU.mult)
                last.then_inc(xn_ready, 1)

            def cut(c, k, w):
                src = (ps_q, ps_k)[w]
                dve.wait_ge(hi_ready, 2 * c + w + 1)
                nc.vector.tensor_tensor(rest[:, w], src, qk_parts[:, k, w, 0], ALU.subtract).then_inc(rest_ready, 1)

            def body(j, n):
                c, k = CPB * j + n, n % 2
                if isinstance(c, int) and c < 0:
                    layernorm(j, n + 2)
                    return
                if not (isinstance(c, int) and c < 1):
                    add_linear(c - 1)
                dve.wait_ge(xnT_ready, c + 1)
                if not (isinstance(c, int) and c < 1):
                    dve.wait_ge(y8_ready, c)
                nc.vector.tensor_scalar(quant[:], xnT[:, k], scales[:, 2:3], FP8_MAX, ALU.mult,
                                        ALU.min).then_inc(quant_chain, 1)
                dve.wait_ge(quant_chain, 3 * c + 1)
                nc.vector.tensor_scalar(quant[:], quant[:], -FP8_MAX, None, ALU.max).then_inc(quant_chain, 1)
                dve.wait_ge(quant_chain, 3 * c + 2)
                nc.vector.tensor_scalar(power[:].bitcast(I32), quant[:].bitcast(I32), 0x7F800000, None,
                                        ALU.bitwise_and).then_inc(quant_chain, 1)
                dve.wait_ge(quant_chain, 3 * c + 3)
                nc.vector.tensor_scalar(power[:], power[:], FP8_MIN_NORMAL, ROUND, ALU.max,
                                        ALU.mult).then_inc(power_ready, 1)
                if isinstance(c, int) and c == 0:
                    prepare_linear()
                cut(c, k, 0)
                layernorm(j, n + 2)
                cut(c, k, 1)
                for w in range(2):
                    dve.wait_ge(mid_ready, 2 * c + w + 1)
                    nc.vector.tensor_tensor(qk_parts[:, k, w, 2], rest[:, w], qk_parts[:, k, w, 1],
                                            ALU.subtract).then_inc(lo_ready, 1)

            layernorm(0, 0)
            dve.wait_ge(scales_loaded, 16 * 4)
            nc.vector.reciprocal(scales[:, 2:3], scales[:, 0:1]).then_inc(bias_ready, 1)
            nc.vector.tensor_tensor(scales[:, 3:4], scales[:, 0:1], scales[:, 1:2], ALU.mult).then_inc(bias_ready, 1)
            nc.vector.tensor_tensor(bias[:], bias[:], bias_o[:], ALU.add).then_inc(bias_ready, 1)
            dve.wait_ge(bias_ready, 3)
            chunks(dve, body)
            add_linear(B * CPB - 1)

        @block.tensor
        def _(pe):
            pe.wait_ge(ident_loaded, 16)

            def body(j, n):
                c = CPB * j + n
                k, k1 = n % 2, (n + 1) % 2
                main = not (isinstance(c, int) and c < 0)
                ahead = not (isinstance(c, int) and c + 1 > B * CPB - 1)
                if main:
                    if isinstance(c, int) and c == 0:
                        pe.wait_ge(w_loaded, 48)
                    pe.wait_ge(xnT_ready, c + 1)
                    if not (isinstance(c, int) and c < 1):
                        pe.wait_ge(rest_ready, 2 * c - 1)
                    for m in range(KC):
                        for i in range(KC):
                            last = nc.tensor.matmul(ps_q[:, m], wq[:, i, m * P:(m + 1) * P], xnT[:, k, i],
                                                    start=(i == 0), stop=(i == KC - 1))
                    last.then_inc(q_ready, 1)
                if ahead:
                    pe.wait_ge(xn_ready, c + 2)
                    if not (isinstance(c, int) and c < 1):
                        pe.wait_ge(base_ready, c)
                    for i in range(KC):
                        for t in range(TT):
                            last = nc.tensor.transpose(ps_t[:, i, t * P:(t + 1) * P],
                                                       xn[:, k1, t, i * P:(i + 1) * P], keep["ident"][:])
                    last.then_inc(t_ready, 1)
                if main:
                    if not (isinstance(c, int) and c < 1):
                        pe.wait_ge(rest_ready, 2 * c)
                    grouped = xnT[:, k].rearrange("p i (g r) -> p i g r", r=STRIDE)
                    ns = CH // STRIDE
                    for m in range(KC):
                        for cols, keys in ((slice(0, ns), grouped[:, :, :, 0]), (slice(ns, CH), grouped[:, :, :, 1:])):
                            for i in range(KC):
                                last = nc.tensor.matmul(ps_k[:, m, cols], wk[:, i, m * P:(m + 1) * P], keys[:, i],
                                                        start=(i == 0), stop=(i == KC - 1))
                    last.then_inc(k_ready, 1)
                    if not (isinstance(c, int) and c < 1):
                        pe.wait_ge(v_copied, c)
                    for t in range(TT):
                        for i in range(KC):
                            last = nc.tensor.matmul(ps_v[:, t // 2, t % 2 * H:(t % 2 + 1) * H],
                                                    xnT[:, k, i, t * P:(t + 1) * P], wv[:, i],
                                                    start=(i == 0), stop=(i == KC - 1))
                    last.then_inc(v_ready, 1)
                    if isinstance(c, int) and c == 0:
                        pe.wait_ge(w8_ready, 1)
                    pe.wait_ge(y8_ready, c + 1)
                    if ahead:
                        pe.wait_ge(xnT_ready, c + 2)
                    else:
                        pe.wait_ge(base_ready, c)
                    for t in range(TT):
                        for i in range(KC):
                            for part in range(2):
                                last = nc.tensor.matmul(ps_f[:, t // 2, t % 2 * H:(t % 2 + 1) * H],
                                                        y8[:, k, i, t * P:(t + 1) * P], w8_parts[:, part, i],
                                                        start=(i == 0 and part == 0),
                                                        stop=(i == KC - 1 and part == 1))
                    last.then_inc(f_ready, 1)

            chunks(pe, body)


ROUNDS = NS // P + 1
SU = ROUNDS * HG
S_BANKS = 4
M_AT = 1
FIRST, LAST = -2, STEPS + 1


def max_units(s):
    units = []
    for r in range(ROUNDS - 1):
        if r == M_AT and -1 <= s and s + 1 < STEPS:
            units.append(("negmax",))
        if s + 2 < STEPS:
            units.append(("window", r))
            units += [("strided", h, r) for h in range(HG)]
    return units


def v_units(s):
    return [u for u in max_units(s) if u[0] != "window"]


def part_attend(nc, dram, keep, out):
    before = {FIRST: 0}
    for s in range(FIRST, LAST + 1):
        before[s + 1] = before[s] + len(v_units(s))

    class Step:

        def __init__(self, j, n):
            self.j, self.n = j, n

        def at(self, d=0):
            return 2 * CPB * self.j + self.n + d

        def exists(self, d=0):
            return not isinstance(self.at(d), int) or 0 <= self.at(d) < STEPS

        def queries(self, d=0):
            return (self.n + d) % CPB

        def iteration(self, d=0):
            return 2 * self.j + (self.n + d) // CPB

        def parity(self, d=0):
            return (self.n + d) // CPB % 2

        def half_iteration(self, d=0):
            return self.j + (self.n + d) // CPB // 2

        def half(self, d=0):
            return CPB * self.j + (self.n + d) // 2

        def units(self):
            return max_units(self.n)

        def unit(self, d, kind):
            units = v_units(self.n + d)
            return 2 * CPB * len(v_units(2)) * self.j + before[self.n + d] + units.index(kind) + 1

        def window(self, h):
            return HG * self.at(2) + h + 1

        def bank_holder(self, i):
            if i >= 3:
                return 0, self.units()[i - 3]
            if self.n - 1 not in before or not max_units(self.n - 1):
                return None
            units = max_units(self.n - 1)
            return -1, units[max(u for u in range(len(units)) if u % 3 == i)]

    def steps(eng, body):
        for n in range(FIRST, 2):
            body(Step(0, n))
        with eng.Fori(0, (STEPS - 8) // 8) as j:
            for n in range(2, 10):
                body(Step(j, n))
        for n in range(STEPS - 6, LAST + 1):
            body(Step(0, n))

    with ExitStack() as ctx:
        def sb(name, shape, dt=F32):
            return ctx.enter_context(nc.sbuf_tensor(name, shape, dt))

        def sem(name):
            return ctx.enter_context(nc.semaphore(name))

        ps = ctx.enter_context(nc.psum_tensor("ps_attend", [P, 8, CH], F32))
        ps_s = [ps[:, i] for i in range(S_BANKS)]
        ps_v = [ps[:, S_BANKS + i] for i in range(3)]
        ps_o = ps[:, S_BANKS + 3]

        q_op = [keep["q_op"], sb("q_op1", [P, HG * S], BF16)]
        k_op = [keep["k_op"], sb("k_op1", [P, HG * S + 2 * WPAD], BF16)]
        v_op = [sb(f"v_op{i}", [P, NS // P + S // P, HG * VW]) for i in range(2)]
        probs = sb("probs", [P, ROUNDS, HG, CH])
        out_rows = sb("out_rows", [P, 2, CH])
        peak = sb("peak", [P, 2, HG, TT])
        windows = sb("windows", [P, 2, TT * WIN])
        top = sb("top", [P, HG, TT])
        top_rest = sb("top_rest", [P, HG, TT])
        negmax = sb("negmax", [P, 2, HG, PARTS, TT], BF16)
        negmax_rows = sb("negmax_rows", [P, 2, P], BF16)
        sums = sb("sums", [P, HG * CH // P])
        shares = sb("shares", [P, HG * CH // P])
        share_rows = sb("share_rows", [P, CH])
        scale = sb("scale", [P, 2])

        tails_set = sem("tails_set")
        ones_set = sem("ones_set")
        scale_ready = sem("scale_ready")
        qk_loaded = keep["qk_loaded"]
        v_loaded = [sem(f"v_loaded{i}") for i in range(2)]
        s_ready = sem("s_ready")
        exp_done = sem("exp_done")
        pv_done = sem("pv_done")
        out_copied = sem("out_copied")
        u_ready = sem("u_ready")
        u_used = sem("u_used")
        w_ready = sem("w_ready")
        w_copied = sem("w_copied")
        w_masked = sem("w_masked")
        w_used = sem("w_used")
        top_chain = sem("top_chain")
        negmax_ready = sem("negmax_ready")
        negmax_stored = sem("negmax_stored")
        negmax_loaded = sem("negmax_loaded")
        sums_stored = sem("sums_stored")
        sums_loaded = sem("sums_loaded")
        shares_ready = sem("shares_ready")
        shares_stored = sem("shares_stored")
        shares_loaded = sem("shares_loaded")
        attn_ready = sem("attn_ready")
        attn_stored = [sem(f"attn_stored{i}") for i in range(2)]
        heads_loaded = [sem(f"heads_loaded{i}") for i in range(CPB)]
        y_ready = sem("y_ready")
        total_ready = sem("total_ready")
        out_stored = sem("out_stored")

        heads = q_op[0][:].bitcast(F32).rearrange("p (n i q) -> p n i q", n=CPB, i=KC)
        ps_y = [ps[:, 2 * i:2 * i + 2] for i in range(CPB)]
        base = keep["base"].rearrange("p (c t) f -> p c (t f)", t=TT)
        out_tiles = out.rearrange("b (c t p) f -> (b c) p t f", t=TT, p=P)

        def load_heads(eng, b, n, i):
            rows = dram["attn"][bass.ds(b * G + 2 * i, 2), :, n * CH:(n + 1) * CH].rearrange(
                "g (h r) s -> (g h) r s", r=VW)
            eng.dma_start(heads[:, n, i], rows[:, 0:D]).then_inc(heads_loaded[n], 16)

        block = ctx.enter_context(nc.Block())

        def window(tile):
            return NS - WPAD + WSTEP * tile

        @block.gpsimd
        def _(pool):
            for par in range(2):
                nc.gpsimd.memset(k_op[par][:, HG * S:], 0.0).then_inc(tails_set, 1)
                pool.wait_ge(tails_set, par + 1)
            def body(st):
                for h in range(HG):
                    if h == 3 and st.n >= 2:
                        par = st.n % 2
                        pool.wait_ge(shares_loaded, 16 * st.at(-1))
                        nc.gpsimd.tensor_tensor(out_rows[:, par], out_rows[:, par], share_rows[:],
                                                ALU.mult).then_inc(attn_ready, 1)
                    if ("window", h) in st.units():
                        mask = {0: 0, CPB - 1: 2}.get(st.queries(2), 1)
                        pool.wait_ge(w_copied, st.window(h))
                        nc.gpsimd.tensor_tensor(windows[:, h % 2], windows[:, h % 2], keep["max_mask"][:, mask],
                                                ALU.add).then_inc(w_masked, 1)
                    if st.n == -1:
                        pool.wait_ge(w_masked, st.window(h))
                        nc.gpsimd.memset(k_op[1][KR:KM, h * S:(h + 1) * S], 1.0).then_inc(ones_set, 1)
                        pool.wait_ge(ones_set, h + 1)

            steps(pool, body)

        @block.sync
        def _(sp):
            def load_v(it, par, windows=range(-1, STRIDE - 1)):
                v = dram["v"][it]
                for r in windows:
                    if r < 0:
                        to, src = v_op[par][:, 0:NS // P, :], v[LOCAL:LOCAL + S, :].rearrange(
                            "(c p r) w -> r p c w", p=P, r=STRIDE)[0]
                    else:
                        to = v_op[par][r:WIN:STRIDE - 1, NS // P:, :]
                        src = bass.AP(tensor=v.tensor, offset=v.offset + (1 + r) * HG * VW,
                                      ap=[[STRIDE * HG * VW, WIN // 3], [P * HG * VW, S // P], [1, HG * VW]])
                    sp.dma_start(to, src).then_inc(v_loaded[par], 16)

            load_v(0, 0)

            def load_piece(st, piece):
                place, it, par = st.queries(), st.iteration(CPB), st.parity(CPB)
                if st.exists() and not st.exists(CPB - place):
                    if place == piece == 0:
                        sp.wait_ge(s_ready, SU * (STEPS - CPB))
                        for k in range(2):
                            sp.wait_ge(attn_stored[k], 16 * G * CPB // 2)
                    load_heads(sp, 0, place, piece)
                elif not st.exists():
                    return
                elif place < 2:
                    if st.n >= CPB and place == piece == 0:
                        sp.wait_ge(s_ready, SU * st.at())
                    load_qk(sp, dram, {"q_op": q_op[par], "k_op": k_op[par], "qk_loaded": qk_loaded}, it, par,
                            ("k_op", "q_op")[place:place + 1], range(4 * piece, 4 + 2 * piece))
                else:
                    if st.n >= CPB and place == 2 and piece == 0:
                        sp.wait_ge(pv_done, ROUNDS * st.at(-2))
                    r = 2 * (place - 2) + piece - 1
                    load_v(it, par, range(r, r + 1))

            def body(st):
                if st.n >= 2:
                    sp.wait_ge(shares_ready, st.at(-1))
                    sp.dma_start(dram["shares"].rearrange("h (p w) -> (h p) w", w=HG * CH // P), shares[:]
                                 ).then_inc(shares_stored, 16)
                    sp.wait_ge(shares_stored, 16 * st.at(-1))
                    sp.dma_start(share_rows[:], dram["shares"].unsqueeze(1).broadcast_to([HG, VW, CH])
                                 ).then_inc(shares_loaded, 16)
                load_piece(st, 0)
                if st.n >= 2:
                    sp.wait_ge(attn_ready, st.at(-1))
                    cols = slice(st.queries(-2) * CH, (st.queries(-2) + 1) * CH)
                    sp.dma_start(dram["attn"][st.iteration(-2), :, cols], out_rows[:, st.n % 2]
                                 ).then_inc(attn_stored[st.n % 2], 16)
                if st.n >= 1 and st.exists(-1):
                    sp.wait_ge(out_copied, st.at())
                    sp.dma_start(dram["sums"], out_rows[D::VW, (st.n - 1) % 2]).then_inc(sums_stored, 16)
                load_piece(st, 1)
                if st.n >= 1 and st.exists(-1):
                    sp.wait_ge(sums_stored, 16 * st.at())
                    sp.dma_start(sums[:], dram["sums"].rearrange("h (p w) -> (h p) w", w=HG * CH // P)
                                 ).then_inc(sums_loaded, 16)

            steps(sp, body)
            with sp.Fori(0, B * CPB) as c:
                sp.wait_ge(total_ready, c + 1)
                sp.dma_start(out_tiles[c], keep["base"].rearrange("p (c t) f -> p c t f", t=TT)[:, c]
                             ).then_inc(out_stored, 16)
            sp.wait_ge(out_stored, 16 * B * CPB)

        @block.scalar
        def _(act):
            nc.scalar.activation(scale[:, 0:1], keep["unity"][:], ACT.Tanh, scale=0.5).then_inc(scale_ready, 1)
            act.wait_ge(scale_ready, 2)

            def copy_out(st):
                act.wait_ge(pv_done, ROUNDS * st.at())
                if st.n >= 3:
                    act.wait_ge(attn_stored[(st.n - 1) % 2], 16 * st.half(-1))
                nc.scalar.activation(out_rows[:, (st.n - 1) % 2], ps_o, ACT.Copy).then_inc(out_copied, 1)

            def body(st):
                for r in range(ROUNDS):
                    if ("window", r) in st.units():
                        act.wait_ge(w_ready, st.window(r))
                        if r >= 2 or st.n > FIRST:
                            act.wait_ge(w_used, st.window(r - 2))
                        nc.scalar.activation(windows[:, r % 2], ps_v[st.units().index(("window", r)) % 3][:, 0:TT * WIN],
                                             ACT.Copy).then_inc(w_copied, 1)
                    for h in range(HG):
                        if st.exists():
                            i = r * HG + h
                            act.wait_ge(s_ready, SU * st.at() + i + 1)
                            if h == 0 and st.n >= 1:
                                act.wait_ge(pv_done, ROUNDS * st.at(-1) + r + 1)
                            rows = P if r < ROUNDS - 1 else WIN
                            nc.scalar.activation(probs[0:rows, r, h], ps_s[i % S_BANKS][0:rows], ACT.Exp,
                                                 scale=scale[0:rows, 1:2]).then_inc(exp_done, 1)
                        if r == 2 and h == 0 and st.exists(-1):
                            copy_out(st)
                        if ("negmax",) in st.units() and r == 2 and h == 0:
                            par = st.n % 2
                            act.wait_ge(u_used, st.unit(0, ("negmax",)))
                            if st.n >= 1:
                                act.wait_ge(negmax_loaded, 16 * st.at(0))
                            act.dma_start(dram["negmax"][par].rearrange("k (t q) -> (k t) q", q=P),
                                          negmax_rows[0:HG * PARTS * TT, par]).then_inc(negmax_stored, 16)
                        if ("negmax",) in st.units() and r == 3 and h == 2:
                            cols = slice(st.queries(1) * CH, (st.queries(1) + 1) * CH)
                            act.wait_ge(negmax_stored, 16 * st.at(2))
                            act.dma_start(
                                q_op[st.parity(1)][KR:KM, :].rearrange("p (h s) -> p h s", h=HG)[:, :, cols],
                                dram["negmax"][st.n % 2].rearrange("(h a) s -> a h s", a=PARTS)
                                ).then_inc(negmax_loaded, 16)

            steps(act, body)
            for k in range(2):
                act.wait_ge(attn_stored[k], 16 * (B - 1) * G * CPB // 2)
            with act.Fori(1, B - 1) as j:
                for n in range(CPB):
                    act.wait_ge(y_ready, CPB * j + n - CPB + 1)
                    for i in range(KC):
                        load_heads(act, j, n, i)
            for n in range(CPB):
                act.wait_ge(y_ready, (B - 2) * CPB + n + 1)
                if n == 0:
                    for k in range(2):
                        act.wait_ge(attn_stored[k], 16 * STEPS // 2)
                for i in range(KC):
                    load_heads(act, B - 1, n, i)

        @block.vector
        def _(dve):
            dve.wait_ge(scale_ready, 1)
            nc.vector.tensor_scalar(scale[:, 1:2], scale[:, 0:1], 0.5 * D ** -0.5, 0.5 * D ** -0.5, ALU.mult,
                                    ALU.add).then_inc(scale_ready, 1)

            def body(st):
                units = st.units()

                def turn_sums():
                    dve.wait_ge(sums_loaded, 16 * st.at(-1))
                    if st.n >= 3:
                        dve.wait_ge(shares_stored, 16 * st.at(-2))
                    nc.vector.reciprocal(shares[:], sums[:]).then_inc(shares_ready, 1)

                def window_peak(h):
                    dve.wait_ge(w_masked, st.window(h))
                    nc.vector.tensor_reduce(
                        peak[:, 1, h], windows[:, h % 2].rearrange("p (t w) -> p t w", t=TT), AX_X, ALU.max
                        ).then_inc(w_used, 1)

                if st.n >= 2 and not units:
                    turn_sums()
                for i, unit in enumerate(units):
                    if unit[0] == "window":
                        if unit[1] > 0:
                            window_peak(unit[1] - 1)
                        continue
                    src = ps_v[i % 3]
                    dve.wait_ge(u_ready, st.unit(0, unit))
                    if unit[0] == "strided":
                        h, tile = unit[1:]
                        ins = nc.vector.tensor_reduce(peak[:, 0, h, tile:tile + 1], src, AX_X, ALU.max)
                    else:
                        if st.n >= 2:
                            turn_sums()
                        par = st.n % 2
                        if st.n >= 1:
                            dve.wait_ge(negmax_stored, 16 * st.at())
                        ins = nc.vector.tensor_copy(negmax_rows[0:HG * PARTS * TT, par],
                                                    src[0:HG * PARTS * TT, 0:P])
                    ins.then_inc(u_used, 1)
                if st.exists(2):
                    window_peak(HG - 1)
                    dve.wait_ge(u_used, st.unit(0, units[-1]))
                    dve.wait_ge(w_used, st.window(HG - 1))
                    done = 4 * st.at(2)
                    parts = negmax[:, st.n % 2]
                    nc.vector.tensor_tensor(top[:], peak[:, 0], peak[:, 1], ALU.max).then_inc(top_chain, 1)
                    dve.wait_ge(top_chain, done + 1)
                    nc.vector.tensor_scalar(parts[:, :, 0], top[:], -1.0, None, ALU.mult).then_inc(top_chain, 1)
                    dve.wait_ge(top_chain, done + 2)
                    nc.vector.scalar_tensor_tensor(top_rest[:], top[:], -1.0, parts[:, :, 0], ALU.mult,
                                                   ALU.subtract).then_inc(top_chain, 1)
                    dve.wait_ge(top_chain, done + 3)
                    nc.vector.tensor_copy(parts[:, :, 1], top_rest[:]).then_inc(top_chain, 1)
                    dve.wait_ge(top_chain, done + 4)
                    nc.vector.tensor_tensor(parts[:, :, 2], top_rest[:], parts[:, :, 1],
                                            ALU.subtract).then_inc(negmax_ready, 1)

            steps(dve, body)
            with dve.Fori(0, B) as j:
                for n in range(CPB):
                    c = CPB * j + n
                    dve.wait_ge(y_ready, c + 1)
                    nc.vector.tensor_tensor(base[:, c], ps_y[n].rearrange("p a f -> p (a f)"), base[:, c],
                                            ALU.add).then_inc(total_ready, 1)

        @block.tensor
        def _(pe):
            def score(st, r, h):
                i = r * HG + h
                q, k, q0 = q_op[st.parity()], k_op[st.parity()], h * S + st.queries() * CH
                if i == 0:
                    pe.wait_ge(negmax_loaded, 16 * st.at(1))
                    if st.n == 1:
                        pe.wait_ge(ones_set, HG)
                if i >= S_BANKS or st.n >= 1:
                    pe.wait_ge(exp_done, SU * st.at() + i - S_BANKS + 1)
                if r < ROUNDS - 1:
                    ins = nc.tensor.matmul(ps_s[i % S_BANKS], k[0:KM, h * S + r * P:h * S + (r + 1) * P],
                                           q[0:KM, q0:q0 + CH], start=True, stop=True)
                else:
                    mask = {0: 0, CPB - 1: 2}.get(st.queries(), 1)
                    nc.tensor.matmul(ps_s[i % S_BANKS][0:WIN], keep["ident_bf"][0:WIN, 0:WIN], keep["key_mask"][0:WIN, mask],
                                     start=True, stop=False)
                    for t in range(TT):
                        at = h * S + window(st.queries() * TT + t)
                        ins = nc.tensor.matmul(ps_s[i % S_BANKS][0:WIN, t * P:(t + 1) * P], k[0:KM, at:at + WIN],
                                               q[0:KM, q0 + t * P:q0 + (t + 1) * P], start=False, stop=(t == TT - 1))
                ins.then_inc(s_ready, 1)

            def unit(st, i, kind, h=None, tile=None):
                bank = ps_v[i % 3]
                holder = st.bank_holder(i)
                if holder and holder[1][0] == "window":
                    pe.wait_ge(w_copied, HG * st.at(holder[0] + 2) + holder[1][1] + 1)
                elif holder:
                    pe.wait_ge(u_used, st.unit(*holder))
                if kind == "negmax":
                    pe.wait_ge(negmax_ready, st.at(2))
                    parts = negmax[:, (st.n + 1) % 2].rearrange("p h a t -> p (h a t)")
                    nc.tensor.matmul(bank[0:HG * PARTS * TT, 0:P], parts, keep["ident_bf"][:],
                                     start=True, stop=True).then_inc(u_ready, 1)
                    return
                q, k = q_op[st.parity(2)], k_op[st.parity(2)]
                q0 = h * S + st.queries(2) * CH
                if kind == "window":
                    if h == 0 and st.queries(2) == 0:
                        pe.wait_ge(qk_loaded[st.parity(2)], 16 * QK_LOADS * (st.half_iteration(2) + 1))
                    for t in range(TT):
                        at = h * S + window(st.queries(2) * TT + t)
                        ins = nc.tensor.matmul(bank[:, t * WIN:(t + 1) * WIN], q[0:KR, q0 + t * P:q0 + (t + 1) * P],
                                               k[0:KR, at:at + WIN], start=True, stop=True)
                    ins.then_inc(w_ready, 1)
                else:
                    nc.tensor.matmul(bank, q[0:KR, q0 + tile * P:q0 + (tile + 1) * P],
                                     k[0:KR, h * S:h * S + NS], start=True, stop=True).then_inc(u_ready, 1)

            def weigh(st, d, r):
                out, v = ps_o, v_op[st.parity(d)]
                if r == 0:
                    if st.queries(d) == 0:
                        pe.wait_ge(v_loaded[st.parity(d)], 64 * (st.half_iteration(d) + 1))
                    if st.n + d >= 1:
                        pe.wait_ge(out_copied, st.at(d))
                if r < ROUNDS - 1:
                    pe.wait_ge(exp_done, SU * st.at(d) + (r + 1) * HG)
                    for h in range(HG):
                        ins = nc.tensor.matmul(out[h * VW:(h + 1) * VW], v[:, r, h * VW:(h + 1) * VW], probs[:, r, h],
                                               start=(r == 0), stop=False)
                else:
                    pe.wait_ge(exp_done, SU * st.at(d + 1))
                    for t in range(TT):
                        tile = NS // P + st.queries(d) * TT + t
                        for h in range(HG):
                            ins = nc.tensor.matmul(out[h * VW:(h + 1) * VW, t * P:(t + 1) * P],
                                                   v[0:WIN, tile, h * VW:(h + 1) * VW],
                                                   probs[0:WIN, r, h, t * P:(t + 1) * P],
                                                   start=False, stop=(t == TT - 1))
                ins.then_inc(pv_done, 1)

            def body(st):
                units = list(enumerate(st.units()))

                def next_unit():
                    i, u = units.pop(0)
                    unit(st, i, *u)

                for r in range(ROUNDS):
                    if r == M_AT and units and units[0][1] == ("negmax",):
                        next_unit()
                    if units and units[0][1] == ("window", r):
                        next_unit()
                    for h in range(HG):
                        if st.exists():
                            score(st, r, h)
                        if units and units[0][1] == ("strided", h, r):
                            next_unit()
                    if r >= 2 and st.exists():
                        weigh(st, 0, r - 2)
                    if r < 2 and st.exists(-1):
                        weigh(st, -1, r + 3)

            def project(j, n):
                c = CPB * j + n
                pe.wait_ge(heads_loaded[n], 16 * KC * (j + 1))
                if not isinstance(c, int):
                    pe.wait_ge(total_ready, c - CPB + 1)
                elif n < 2:
                    pe.wait_ge(exp_done, SU * STEPS)
                else:
                    pe.wait_ge(u_used, before[LAST + 1])
                    pe.wait_ge(out_copied, STEPS)
                for t in range(TT):
                    for i in range(KC):
                        last = nc.tensor.matmul(ps_y[n][:, t // 2, t % 2 * H:(t % 2 + 1) * H],
                                                heads[:, n, i, t * P:(t + 1) * P], keep["wo"][:, i],
                                                start=(i == 0), stop=(i == KC - 1))
                last.then_inc(y_ready, 1)

            pe.wait_ge(tails_set, 2)
            steps(pe, body)
            for n in range(CPB):
                project(0, n)
            with pe.Fori(1, B) as j:
                for n in range(CPB):
                    project(j, n)


def build(nc, io, out):
    dram = {
        "qk": [nc.dram_tensor(f"{n}_parts_dram", [PARTS, NIT, HG * D, S], BF16).ap() for n in "qk"],
        "v": nc.dram_tensor("v_dram", [NIT, LOCAL + S + LOCAL, HG * VW], F32).ap(),
        "attn": nc.dram_tensor("attn_dram", [NIT, HG * VW, S], F32).ap(),
        "sums": nc.dram_tensor("sums_dram", [HG, CH], F32).ap(),
        "shares": nc.dram_tensor("shares_dram", [HG, CH], F32).ap(),
        "negmax": nc.dram_tensor("negmax_dram", [2, HG * PARTS, CH], BF16).ap(),
    }
    with ExitStack() as ctx:
        def sb(name, shape, dt=F32):
            return ctx.enter_context(nc.sbuf_tensor(name, shape, dt))

        keep = {
            "ident": sb("ident", [P, P]),
            "ident_bf": sb("ident_bf", [P, P], BF16),
            "max_mask": sb("max_mask", [P, MASKS, TT * WIN], BF16),
            "key_mask": sb("key_mask", [P, MASKS, CH], BF16),
            "base": sb("base", [P, B * S // P, H]),
            "q_op": sb("q_op0", [P, HG * S], BF16),
            "k_op": sb("k_op0", [P, HG * S + 2 * WPAD], BF16),
            "qk_loaded": [ctx.enter_context(nc.semaphore(f"qk_loaded{i}")) for i in range(2)],
            "wo": sb("wo", [P, KC, H]),
            "unity": sb("unity", [P, 1]),
        }
        part_project(nc, io, dram, keep)
        part_attend(nc, dram, keep, out)


def kernel(L0_attn_x, L0_attn_q_w, L0_attn_k_w, L0_attn_v_w, L0_attn_o_w, L0_attn_o_b, L0_attn_unity_scale,
           L0_ffn_weight_fp8, L0_ffn_bias, L0_ffn_input_scale, L0_ffn_weight_scale):
    import numpy as np
    import concourse.bacc as bacc
    from concourse.bass_utils import run_bass_kernel_spmd

    q = np.arange(P)
    key = np.arange(WIN)
    rel = STRIDE * (key // 3) + 1 + key % 3 - LOCAL
    near = np.abs(rel[:, None] - q[None, :]) <= LOCAL
    seen = np.stack([np.stack([near] * TT, 1)] * MASKS)
    seen[0, :, 0] &= (rel >= 0)[:, None]
    seen[MASKS - 1, :, TT - 1] &= (rel < P)[:, None]
    key_mask = np.where(seen, np.float32(0), np.float32(-BIG)).reshape(MASKS, WIN, CH)
    max_mask = np.where(seen.transpose(0, 3, 2, 1), np.float32(0), np.float32(-BIG)).reshape(MASKS, P, TT * WIN)

    def columns(w):
        w = np.asarray(w).reshape(H, KC, G // KC, HG, D)
        return np.ascontiguousarray(w.transpose(0, 1, 2, 4, 3)).reshape(H, H)

    arrays = {
        "x": np.asarray(L0_attn_x),
        "q_w": columns(L0_attn_q_w),
        "k_w": columns(L0_attn_k_w),
        "v_w": np.asarray(L0_attn_v_w),
        "o_w": np.asarray(L0_attn_o_w),
        "o_b": np.asarray(L0_attn_o_b),
        "unity": np.asarray(L0_attn_unity_scale).reshape(1),
        "w8T": np.ascontiguousarray(np.asarray(L0_ffn_weight_fp8).T),
        "ffn_bias": np.asarray(L0_ffn_bias),
        "input_scale": np.asarray(L0_ffn_input_scale),
        "weight_scale": np.asarray(L0_ffn_weight_scale),
        "ident": np.eye(P, dtype=np.float32),
        "max_mask": np.ascontiguousarray(max_mask),
        "key_mask": np.ascontiguousarray(key_mask),
    }
    nc = bacc.Bacc("TRN2", target_bir_lowering=False, num_devices=1)
    io = {n: nc.dram_tensor(f"in_{n}", a.shape, mybir.dt.from_np(a.dtype), kind="ExternalInput").ap()
          for n, a in arrays.items()}
    out = nc.dram_tensor("out", [B, S, H], F32, kind="ExternalOutput").ap()
    build(nc, io, out)
    r = run_bass_kernel_spmd(nc, [{f"in_{n}": a for n, a in arrays.items()}], core_ids=[0])
    return r.results[0]["out"]
```
